# Optimizing a Trainium2 kernel written in Bass

```python
import numpy as np
import jax
import jax.numpy as jnp

def _softmax(x, axis=-1):
    return jax.nn.softmax(x, axis=axis)

def _gelu(x):
    return jax.nn.gelu(x, approximate=True)

def _silu(x):
    return jax.nn.silu(x)

def _sigmoid(x):
    return jax.nn.sigmoid(x)

def _layernorm(x, axis=-1, eps=1e-05):
    m = jnp.mean(x, axis=axis, keepdims=True)
    v = jnp.var(x, axis=axis, keepdims=True)
    return (x - m) / jnp.sqrt(v + eps)

def _scatter_add(tgt, idx, src, axis=0):
    return tgt.at[idx].add(src)

def _segment_sum(src, seg, n):
    return jax.ops.segment_sum(src, seg, n)
kernel_name = 'mk_seq_preln_d1_jaxref_r8_162375'

def setup_inputs(seed: int=0):
    np.random.seed(seed)
    _w = jnp.asarray

    def _L0_attn_setup():
        import math
        import jax, jax.numpy as jnp
        import numpy as np
        D_MODEL = 128
        N_HEADS = 16
        D_K = D_MODEL // N_HEADS
        D_C = 32
        B, S = (2, 256)
        key = jax.random.key(seed)
        ks = jax.random.split(key, 7)
        sd = lambda fan_in: 1.0 / math.sqrt(fan_in)
        return {'x': jax.random.normal(ks[0], (B, S, D_MODEL), dtype=jnp.float32), 'W_dq': jax.random.uniform(ks[1], (D_MODEL, D_C), minval=-sd(D_MODEL), maxval=sd(D_MODEL), dtype=jnp.float32), 'W_uq': jax.random.uniform(ks[2], (D_C, N_HEADS * D_K), minval=-sd(D_C), maxval=sd(D_C), dtype=jnp.float32), 'W_dkv': jax.random.uniform(ks[3], (D_MODEL, D_C), minval=-sd(D_MODEL), maxval=sd(D_MODEL), dtype=jnp.float32), 'W_uk': jax.random.uniform(ks[4], (D_C, N_HEADS * D_K), minval=-sd(D_C), maxval=sd(D_C), dtype=jnp.float32), 'W_uv': jax.random.uniform(ks[5], (D_C, N_HEADS * D_K), minval=-sd(D_C), maxval=sd(D_C), dtype=jnp.float32), 'W_o': jax.random.uniform(ks[6], (N_HEADS * D_K, D_MODEL), minval=-sd(N_HEADS * D_K), maxval=sd(N_HEADS * D_K), dtype=jnp.float32)}
    _L0_attn_in = _L0_attn_setup()

    def _L0_ffn_setup():
        import jax, jax.numpy as jnp
        import numpy as np
        B, S, D = (4, 256, 128)
        O = 128
        E = 8
        K = 2
        key = jax.random.key(seed)
        k1, k2, k3, k4, k5 = jax.random.split(key, 5)
        scale = 1.0 / np.sqrt(D)
        x = jax.random.normal(k1, (B, S, D), dtype=jnp.float32)
        We = jax.random.uniform(k2, (E, D, O), dtype=jnp.float32, minval=-scale, maxval=scale)
        be = jax.random.uniform(k3, (E, O), dtype=jnp.float32, minval=-scale, maxval=scale)
        Wg = jax.random.uniform(k4, (D, E), dtype=jnp.float32, minval=-scale, maxval=scale)
        bg = jax.random.uniform(k5, (E,), dtype=jnp.float32, minval=-scale, maxval=scale)
        return {'x': x, 'We': We, 'be': be, 'Wg': Wg, 'bg': bg}
    _L0_ffn_in = _L0_ffn_setup()
    _d = {'L0_attn_x': _L0_attn_in['x'], 'L0_attn_W_dq': _L0_attn_in['W_dq'], 'L0_attn_W_uq': _L0_attn_in['W_uq'], 'L0_attn_W_dkv': _L0_attn_in['W_dkv'], 'L0_attn_W_uk': _L0_attn_in['W_uk'], 'L0_attn_W_uv': _L0_attn_in['W_uv'], 'L0_attn_W_o': _L0_attn_in['W_o'], 'L0_ffn_We': _L0_ffn_in['We'], 'L0_ffn_be': _L0_ffn_in['be'], 'L0_ffn_Wg': _L0_ffn_in['Wg'], 'L0_ffn_bg': _L0_ffn_in['bg']}
    _x0 = _d['L0_attn_x']
    _d['L0_attn_x'] = jax.random.normal(jax.random.fold_in(jax.random.key(seed), 1), (4, 512, 128), dtype=_x0.dtype)
    del _x0
    return _d

def reference(L0_attn_x, L0_attn_W_dq, L0_attn_W_uq, L0_attn_W_dkv, L0_attn_W_uk, L0_attn_W_uv, L0_attn_W_o, L0_ffn_We, L0_ffn_be, L0_ffn_Wg, L0_ffn_bg):

    def _L0_attn_ref(x, W_dq, W_uq, W_dkv, W_uk, W_uv, W_o):
        import math
        import jax, jax.numpy as jnp
        import numpy as np
        D_MODEL = 128
        N_HEADS = 16
        D_K = D_MODEL // N_HEADS
        D_C = 32
        B, S = (2, 256)
        Bx, Sx, _ = x.shape
        c_q = x @ W_dq
        Q = (c_q @ W_uq).reshape(Bx, Sx, N_HEADS, D_K)
        c_kv = x @ W_dkv
        K = (c_kv @ W_uk).reshape(Bx, Sx, N_HEADS, D_K)
        V = (c_kv @ W_uv).reshape(Bx, Sx, N_HEADS, D_K)
        scores = jnp.einsum('bqhd,bkhd->bhqk', Q, K) / math.sqrt(D_K)
        causal = jnp.tril(jnp.ones((Sx, Sx), dtype=bool))
        scores = jnp.where(causal, scores, -jnp.inf)
        attn = jax.nn.softmax(scores, axis=-1)
        out = jnp.einsum('bhqk,bkhd->bqhd', attn, V).reshape(Bx, Sx, N_HEADS * D_K)
        return out @ W_o

    def _L0_ffn_ref(x, We, be, Wg, bg):
        import jax, jax.numpy as jnp
        import numpy as np
        B, S, D = (4, 256, 128)
        O = 128
        E = 8
        K = 2
        b, s, d = x.shape
        x_flat = x.reshape(-1, d)
        gates = jax.nn.softmax(x_flat @ Wg + bg, axis=-1)
        topk_gates, topk_idx = jax.lax.top_k(gates, K)
        topk_gates = topk_gates / jnp.sum(topk_gates, axis=1, keepdims=True)
        expert_out = jnp.einsum('nd,edo->neo', x_flat, We) + be
        selected = jnp.take_along_axis(expert_out, topk_idx[:, :, None], axis=1)
        out = jnp.sum(selected * topk_gates[:, :, None], axis=1)
        return out.reshape(b, s, -1)
    x = L0_attn_x
    x = x + _L0_attn_ref(_layernorm(x, axis=-1), L0_attn_W_dq, L0_attn_W_uq, L0_attn_W_dkv, L0_attn_W_uk, L0_attn_W_uv, L0_attn_W_o)
    x = x + _L0_ffn_ref(_layernorm(x, axis=-1), L0_ffn_We, L0_ffn_be, L0_ffn_Wg, L0_ffn_bg)
    return x

_drawn_inputs = setup_inputs


def setup_inputs(seed=0):
    import zlib

    import numpy as np

    out = dict(_drawn_inputs(seed))
    spreads = {}
    factors = {'L0_attn_W_dq': 3.379, 'L0_attn_W_uq': 2.894, 'L0_attn_W_uk': 2.817}
    for name, (base, spread) in spreads.items():
        noise = np.random.default_rng([zlib.crc32(name.encode()), seed]).standard_normal(out[name].shape)
        drawn = base * np.exp(spread * noise) if base else spread * noise
        out[name] = jnp.asarray(drawn.astype(out[name].dtype))
    for name, factor in factors.items():
        out[name] = (out[name] * factor).astype(out[name].dtype)
    return out
```

```python
from contextlib import ExitStack

import concourse.bass as bass
from concourse import mybir

F32 = mybir.dt.float32
BF16 = mybir.dt.bfloat16
U32 = mybir.dt.uint32
ALU = mybir.AluOpType
ACT = mybir.ActivationFunctionType
AX = mybir.AxisListType

P = 128
SUB = 64
EPS = 1e-5
BIG = 1e30
PARTS = ((0, 0), (0, 1), (1, 0), (0, 2), (2, 0), (1, 1))

AT_XT, AT_C, AT_Q, AT_K, AT_V = 0, 1, 3, 4, 6
LAG = 6
AT_OT0, AT_OT1, AT_ONT, AT_Y, AT_X2T, AT_LOG, AT_GT, AT_BIAS = 8, 9, 11, 12, 16, 17, 20, 21
AT_MOE, AT_LN1 = 1, 20


def fill_plan(SUBS, bank):
    plan = []
    for c in range(SUBS, 0, -1):
        m = min(4, bank // (SUB * c))
        m = 4 if m == 3 else m
        m = 2 if m == 2 else m
        for j in range(0, 4, m):
            plan.append((c, j, m))
    return plan


def build(nc, x, W_dq, W_uq, W_dkv, W_uk, W_uv, W_o, We, be, Wg, bg, out):
    B, S, D = x.shape
    C = W_dq.shape[1]
    NE, _, DO = We.shape
    H = 16
    DK = D // H
    T = S // P
    I = S // SUB
    NP = H // 2
    NU = 2 * B
    SCALE = float(DK) ** -0.5
    FILLS = fill_plan(I, S)
    NF = len(FILLS)
    NMF = NF + 1
    NDMA = len(PARTS) * 2 + 1

    with ExitStack() as ctx:
        def sb(name, shape, dt):
            return ctx.enter_context(nc.sbuf_tensor(name, shape, dt))

        def pb(name):
            return ctx.enter_context(nc.psum_tensor(name, [P, 512], F32))

        def sem(name):
            return ctx.enter_context(nc.semaphore(name))

        QS = sb("QS", [P, 2, H, S], BF16)
        KS = sb("KS", [P, 2, H, S], BF16)
        VB = sb("VB", [P, 2, I, NP, 32], F32)
        PR = sb("PR", [P, 2, 4, S], F32)
        X = sb("X", [P, B, T, D], F32)
        TOK = sb("TOK", [P, B, T, D], F32)
        FT = sb("FT", [P, B, T, P], F32)
        CT = sb("CT", [2 * C, B, S], F32)
        OT = sb("OT", [P, B, 2, S], F32)
        PT1 = sb("PT1", [P, 2, 2, S], BF16)
        PT2 = sb("PT2", [P, 2, 2, S], BF16)
        PT3 = sb("PT3", [P, 2, 2, S], BF16)
        RES = sb("RES", [P, 2, 2, S], F32)
        MX = sb("MX", [P, 2, 4, I], F32)
        SH = sb("SH", [4 * I, 2, 2, P], BF16)
        Wd = sb("Wd", [P, 2 * C], F32)
        Wu = sb("Wu", [2 * C, 2, P], F32)
        WP = sb("WP", [2 * C, P], F32)
        Wo = sb("Wo", [P, D], F32)
        WE = sb("WE", [P, NE, DO], F32)
        BE = sb("BE", [NE, DO], F32)
        WG = sb("WG", [P, NE], F32)
        BG = sb("BG", [P, NE], F32)
        ident = sb("ident", [P, P], F32)
        identb = sb("identb", [P, P], BF16)
        MSK = sb("MSK", [P, 2, SUB], BF16)
        ZR = sb("ZR", [P, S], BF16)
        ON = sb("ON", [P, S], BF16)
        mhalf = sb("mhalf", [P, T], F32)
        iota8 = sb("iota8", [P, NE], F32)
        ST6 = sb("ST6", [P, 2, B, T, 6], F32)
        MV = sb("MV", [P, 2, B, T, 2], F32)
        VE = sb("VE", [P, 2, B, T], F32)
        RS = sb("RS", [P, 2, B, T], F32)
        RL = sb("RL", [P, B, 2, 16, 2], F32)
        LG = sb("LG", [P, B, T, NE], F32)
        TOP = sb("TOP", [P, B, T, 8], F32)
        TIX = sb("TIX", [P, B, T, 8], U32)
        TIF = sb("TIF", [P, B, T, 2], F32)
        DF = sb("DF", [P, B, T], F32)
        E1 = sb("E1", [P, B, T], F32)
        DEN = sb("DEN", [P, B, T], F32)
        G12 = sb("G12", [P, B, 2, T], F32)
        OH = sb("OH", [P, B, 2, T, NE], F32)
        GW = sb("GW", [P, B, 2, T, NE], F32)
        G = sb("G", [P, B, T, NE], F32)
        GT = sb("GT", [NE, B, S], F32)
        PROD = sb("PROD", [P, 2, NE, DO], F32)
        SUM4 = sb("SUM4", [P, 4, DO], F32)
        SUM2 = sb("SUM2", [P, 2, DO], F32)
        SUM1 = sb("SUM1", [P, DO], F32)

        SM = [pb("SM0"), pb("SM1")]
        SA = [pb("SA0"), pb("SA1")]
        PV = pb("PV")
        MA = pb("MA")
        MB = pb("MB")
        ME = pb("ME")

        s_w = sem("weights_in")
        s_wp = sem("up_weights_permuted")
        s_x = [sem(f"x_in{b}") for b in range(B)]
        s_const = sem("constants_made")
        s_on1 = sem("one_rows_made")
        s_vz = sem("value_zeros_made")
        s_vone = sem("value_ones_made")
        s_pad = sem("pad_rows_in")
        s_zero = [sem("zero_rows_made0"), sem("zero_rows_made1")]
        s_st = [sem("ln1_stats"), sem("ln2_stats")]
        s_mv = [sem("ln1_meanvar"), sem("ln2_meanvar")]
        s_ve = [sem("ln1_var_eps"), sem("ln2_var_eps")]
        s_rs = [sem("ln1_rstd"), sem("ln2_rstd")]
        s_ln = [sem("ln1_out"), sem("ln2_out")]
        s_xtp = sem("xT_in_psum")
        s_xt = sem("xT_copied")
        s_cp = sem("c_in_psum")
        s_c = sem("c_copied")
        s_pp = [sem("q_in_psum"), sem("k_in_psum")]
        s_p1 = [sem("q_part1"), sem("k_part1")]
        s_r = [sem("q_rest"), sem("k_rest")]
        s_p2 = [sem("q_part2"), sem("k_part2")]
        s_p3 = [sem("q_part3"), sem("k_part3")]
        s_vp = sem("v_in_psum")
        s_v = sem("v_copied")
        s_qs = [sem("stacked_in0"), sem("stacked_in1")]
        s_smf = sem("max_bank_filled")
        s_smr = sem("max_bank_read")
        s_hi = sem("shift_high")
        s_sh = [sem("shift_rows_in0"), sem("shift_rows_in1")]
        s_saf = sem("att_bank_filled")
        s_exp = sem("exp_done")
        s_pv = sem("pv_done")
        s_ot = sem("pv_copied")
        s_otp = sem("oT_in_psum")
        s_rl = sem("recip_done")
        s_on = sem("o_normalised")
        s_ontp = sem("onT_in_psum")
        s_ont = sem("onT_copied")
        s_yp = sem("y_in_psum")
        s_x1 = sem("x1_done")
        s_x2tp = sem("x2T_in_psum")
        s_x2t = sem("x2T_copied")
        s_lgp = sem("logits_in_psum")
        s_lg = sem("logits_done")
        s_top = sem("top8_done")
        s_tix = sem("top8_index_done")
        s_df = sem("top_difference")
        s_e1 = sem("top_exp")
        s_gate = sem("gate_steps")
        s_g = sem("gates_done")
        s_gtp = sem("gT_in_psum")
        s_gt = sem("gT_copied")
        s_bp = sem("bias_in_psum")
        s_xb = sem("x1_plus_bias")
        s_mep = [sem("experts_lo_in_psum"), sem("experts_hi_in_psum")]
        s_me = [sem("experts_lo_weighted"), sem("experts_hi_weighted")]
        s_sum = sem("expert_sums")
        s_o = sem("tile_out")
        s_store = sem("stored")

        block = ctx.enter_context(nc.Block())

        def stacked(b):
            return 16 * NDMA * (b // 2 + 1)

        @block.sync
        def _(sp):
            for b in range(B):
                sp.dma_start(X[:, b, :, :], x[b].rearrange("(t p) d -> p t d", p=P)).then_inc(s_x[b], 16)
                if b == 0:
                    sp.dma_start(Wd[:, 0:C], W_dq).then_inc(s_w, 16)
                    sp.dma_start(Wd[:, C:2 * C], W_dkv).then_inc(s_w, 16)
                    sp.dma_start(Wu[0:C, 0, :], W_uq).then_inc(s_w, 16)
                    sp.dma_start(Wu[C:2 * C, 0, :], W_uk).then_inc(s_w, 16)
                    sp.dma_start(Wu[C:2 * C, 1, :], W_uv).then_inc(s_w, 16)
            sp.wait_ge(s_on1, 1)
            for par in range(2):
                sp.dma_start(QS[120:128, par, :, :], ZR[:, :]).then_inc(s_pad, 16)
                sp.dma_start(KS[112:120, par, :, :], ON[:, :]).then_inc(s_pad, 16)
                sp.dma_start(KS[120:128, par, :, :], ZR[:, :]).then_inc(s_pad, 16)

            def zero_rows(par):
                for o in range(2):
                    sp.dma_start((QS, KS)[o][0:64, par, :, :],
                                 ZR[0:64, :].unsqueeze(1).to_broadcast([64, H, S])).then_inc(s_zero[par], 16)

            def stack(b):
                if b >= 2:
                    sp.wait_ge(s_saf, NF * 2 * (b - 1))
                sp.dma_start(QS[112:120, b % 2, :, :], ZR[:, :]).then_inc(s_qs[b % 2], 16)
                for level in range(3):
                    for o in range(2):
                        sp.wait_ge((s_p1, s_p2, s_p3)[level][o], b + 1)
                        src = (PT1, PT2, PT3)[level][:, b % 2, o, :]
                        for n, pair in enumerate(PARTS):
                            if pair[o] == level:
                                r = 64 + 8 * n
                                sp.dma_start((QS, KS)[o][r:r + 8, b % 2, :, :], src).then_inc(s_qs[b % 2], 16)

            def shift_rows(u):
                sp.wait_ge(s_smr, NMF * (u + 1))
                g = u % 2
                for part in range(2):
                    for s in range(2):
                        h = NP * s + 4 * g
                        sp.dma_start(QS[112 + part:113 + part, (u // 2) % 2, h:h + 4, :], SH[:, u % 2, part, SUB * s:SUB * s + SUB]).then_inc(s_sh[u % 2], 16)

            def store(b):
                for t in range(T):
                    sp.wait_ge(s_o, T * b + t + 1)
                    sp.dma_start(out[b, t * P:(t + 1) * P, :], TOK[:, b, t, :]).then_inc(s_store, 16)

            stack(0)
            zero_rows(1)
            for u in range(-1, NU):
                b = u // 2
                if u % 2 == 0 and b + 1 < B:
                    stack(b + 1)
                if u % 2 == 1 and b >= 1:
                    store(b - 1)
                if u + 1 < NU:
                    shift_rows(u + 1)
            store(B - 1)
            sp.wait_ge(s_store, 16 * B * T)

        @block.gpsimd
        def _(pool):
            pool.memset(ZR[:, :], 0.0).then_inc(s_const, 1)
            pool.memset(ON[:, :], 0.0).then_inc(s_const, 1)
            pool.memset(ident[:, :], 0.0).then_inc(s_const, 1)
            pool.memset(mhalf[:, :], -0.5).then_inc(s_const, 1)
            pool.wait_ge(s_const, 4)
            pool.memset(ON[0:32, :], 1.0).then_inc(s_on1, 1)
            pool.wait_ge(s_on1, 1)
            pool.affine_select(out=ident[:, :], in_=ident[:, :], compare_op=ALU.not_equal, fill=1.0, base=0,
                               pattern=[[-1, P]], channel_multiplier=1).then_inc(s_const, 1)
            pool.affine_select(out=identb[:, :], in_=ZR[:, 0:P], compare_op=ALU.not_equal, fill=1.0, base=0,
                               pattern=[[-1, P]], channel_multiplier=1).then_inc(s_const, 1)
            for o, sign in ((0, 1), (1, -1)):
                pool.affine_select(out=MSK[:, o, :], in_=ZR[:, 0:SUB], compare_op=ALU.is_ge, fill=-BIG,
                                   base=-SUB * sign, pattern=[[-sign, SUB]],
                                   channel_multiplier=sign).then_inc(s_const, 1)
            pool.wait_ge(s_const, 8)
            for o, sign in ((0, 1), (1, -1)):
                pool.affine_select(out=MSK[0:SUB, o, :], in_=ZR[0:SUB, 0:SUB], compare_op=ALU.is_ge, fill=-BIG,
                                   base=0, pattern=[[-sign, SUB]], channel_multiplier=sign).then_inc(s_const, 1)
            pool.wait_ge(s_const, 10)
            pool.iota(iota8[:, :], pattern=[[1, NE]], base=0, channel_multiplier=0,
                      allow_small_or_imprecise_dtypes=True).then_inc(s_const, 1)

            def rstd(k, b):
                pool.wait_ge(s_ve[k], b + 1)
                pool.tensor_tensor(RS[:, k, b, :], VE[:, k, b, :], mhalf[:, :], ALU.pow).then_inc(s_rs[k], 1)

            def third_parts(b):
                for o in range(2):
                    pool.wait_ge(s_p2[o], b + 1)
                    if b >= 2:
                        pool.wait_ge(s_qs[b % 2], stacked(b - 2))
                    pool.tensor_tensor(PT3[:, b % 2, o, :], RES[:, b % 2, o, :], PT2[:, b % 2, o, :],
                                       ALU.subtract).then_inc(s_p3[o], 1)

            def expert_sums(b, t):
                n = T * b + t
                pr = PROD[:, n % 2, :, :]
                pool.wait_ge(s_me[0], n + 1)
                pool.wait_ge(s_me[1], n + 1)
                pool.tensor_tensor(SUM4[:, :, :], pr[:, 0:4, :], pr[:, 4:8, :], ALU.add).then_inc(s_sum, 1)
                pool.wait_ge(s_sum, 3 * n + 1)
                pool.tensor_tensor(SUM2[:, :, :], SUM4[:, 0:2, :], SUM4[:, 2:4, :], ALU.add).then_inc(s_sum, 1)
                pool.wait_ge(s_sum, 3 * n + 2)
                pool.tensor_tensor(SUM1[:, :], SUM2[:, 0, :], SUM2[:, 1, :], ALU.add).then_inc(s_sum, 1)
                pool.wait_ge(s_sum, 3 * n + 3)
                pool.wait_ge(s_xb, b + 1)
                pool.tensor_tensor(TOK[:, b, t, :], SUM1[:, :], X[:, b, t, :], ALU.add).then_inc(s_o, 1)
                pool.wait_ge(s_o, n + 1)

            rstd(0, 0)
            pool.memset(VB[:, :, :, :, :], 0.0).then_inc(s_vz, 1)
            pool.wait_ge(s_vz, 1)
            pool.memset(VB[0:SUB, :, :, :, 2 * DK:2 * DK + 1], 1.0).then_inc(s_vone, 1)
            pool.wait_ge(s_vone, 1)
            pool.memset(VB[SUB:P, :, :, :, 2 * DK + 1:2 * DK + 2], 1.0).then_inc(s_vone, 1)
            pool.wait_ge(s_vone, 2)
            third_parts(0)
            for u in range(-1, NU):
                b = u // 2
                if u % 2 == 0:
                    if b + 1 < B:
                        third_parts(b + 1)
                    if b >= 1:
                        rstd(1, b - 1)
                else:
                    if b >= 1:
                        for t in range(T):
                            expert_sums(b - 1, t)
                    if b + 2 < B:
                        rstd(0, b + 2)
            rstd(1, B - 1)
            for t in range(T):
                expert_sums(B - 1, t)

        @block.tensor
        def _(pe):
            def xT(b):
                pe.wait_ge(s_const, 5)
                pe.wait_ge(s_ln[0], T * (b + 1))
                if b >= 1:
                    pe.wait_ge(s_v, 2 * b)
                for t in range(T):
                    last = pe.transpose(MA[:, t * P:(t + 1) * P], TOK[:, b, t, :], ident[:, :])
                last.then_inc(s_xtp, 1)

            def down(b):
                pe.wait_ge(s_w, 16 * 10)
                pe.wait_ge(s_xt, b + 1)
                pe.matmul(MA[0:2 * C, :], Wd[:, :], FT[:, b, :, :].rearrange("p t n -> p (t n)"),
                          start=True, stop=True).then_inc(s_cp, 1)

            def up(b, o):
                pe.wait_ge(s_c, b + 1)
                if o == 1 and b >= 3:
                    pe.wait_ge(s_me[0], T * (b - 2))
                pe.wait_ge(s_wp, 1)
                pe.matmul((MA, ME)[o][:, :], WP[C * o:C * o + C, :], CT[C * o:C * o + C, b, :], start=True, stop=True).then_inc(s_pp[o], 1)

            def values(b):
                pe.wait_ge(s_r[0], b + 1)
                w = Wu[C:2 * C, 1, :].rearrange("k (p s e) -> k s p e", s=2, e=DK)
                for i in range(I):
                    for s in range(2):
                        last = pe.matmul(MA[SUB * s:SUB * s + SUB, SUB * i:SUB * i + SUB],
                                         CT[C:2 * C, b, SUB * i:SUB * i + SUB], w[:, s], start=True, stop=True)
                last.then_inc(s_vp, 1)

            def max_fill(u, n):
                b, g, F = u // 2, u % 2, NMF * u + n
                if n == 0 and g == 0:
                    pe.wait_ge(s_qs[b % 2], stacked(b))
                    pe.wait_ge(s_zero[b % 2], 32 if b % 2 else 2)
                    pe.wait_ge(s_const, 10)
                    pe.wait_ge(s_pad, 96)
                if F >= 2:
                    pe.wait_ge(s_smr, F - 1)
                c, j0, m = FILLS[n]
                i, bank = c - 1, SM[F % 2]
                for j in range(m):
                    for s in range(2):
                        h = NP * s + 4 * g + j0 + j
                        pe.matmul(bank[SUB * s:SUB * s + SUB, SUB * c * j:SUB * c * (j + 1)],
                                  QS[:, b % 2, h, SUB * i:SUB * c], KS[:, b % 2, h, 0:SUB * c],
                                  start=(j == 0), stop=False, skip_group_check=True)
                last = pe.matmul(bank[:, 0:m * SUB * c].rearrange("p (j w) -> p j w", j=m)[:, :, SUB * i:SUB * c],
                                 identb[:, :], MSK[:, 0, :].unsqueeze(1).to_broadcast([P, m, SUB]),
                                 start=False, stop=True, skip_group_check=True)
                last.then_inc(s_smf, 1)

            def max_turn(u):
                F = NMF * u + NF
                pe.wait_ge(s_smr, F)
                pe.transpose(SM[F % 2][0:4 * I, 0:P], MX[:, u % 2, :, :].rearrange("p j i -> p (j i)"),
                             ident[:, :]).then_inc(s_smf, 1)

            def att_fill(u, n):
                b, g, F = u // 2, u % 2, NF * u + n
                if n == 0:
                    pe.wait_ge(s_sh[u % 2], 64 * (u // 2 + 1))
                if F >= 2:
                    pe.wait_ge(s_exp, F - 1)
                c, j0, m = FILLS[n]
                i, bank = I - c, SA[F % 2]
                for j in range(m):
                    for s in range(2):
                        h = NP * s + 4 * g + j0 + j
                        pe.matmul(bank[SUB * s:SUB * s + SUB, SUB * c * j:SUB * c * (j + 1)],
                                  KS[:, b % 2, h, SUB * i:SUB * i + SUB], QS[:, b % 2, h, SUB * i:S],
                                  start=(j == 0), stop=False, skip_group_check=True)
                last = pe.matmul(bank[:, 0:m * SUB * c].rearrange("p (j w) -> p j w", j=m)[:, :, 0:SUB],
                                 identb[:, :], MSK[:, 1, :].unsqueeze(1).to_broadcast([P, m, SUB]),
                                 start=False, stop=True, skip_group_check=True)
                last.then_inc(s_saf, 1)

            def pv(u, i):
                b, g = u // 2, u % 2
                done = sum(1 for c, _, _ in FILLS if I - c <= i)
                pe.wait_ge(s_exp, NF * u + done)
                if i == 0:
                    pe.wait_ge(s_v, 2 * (b + 1))
                    pe.wait_ge(s_vone, 2)
                    if u >= 1:
                        pe.wait_ge(s_ot, u)
                for j in range(4):
                    last = pe.matmul(PV[32 * j:32 * j + 32, SUB * i:S], VB[:, b % 2, i, 4 * g + j, :],
                                     PR[:, i % 2, j, 0:S - SUB * i], start=(i == 0), stop=(i == I - 1))
                last.then_inc(s_pv, 1)

            def oT(b, half):
                pe.wait_ge(s_ot, 2 * b + 2)
                if half:
                    pe.wait_ge(s_on, 2 * b + 1)
                elif b >= 1:
                    pe.wait_ge(s_me[1], T * b)
                for tt in range(2):
                    t = 2 * half + tt
                    for g in range(2):
                        last = pe.transpose(MB[:, (2 * tt + g) * P:(2 * tt + g + 1) * P],
                                            OT[:, b, g, t * P:(t + 1) * P], ident[:, :])
                last.then_inc(s_otp, 1)

            def onT(b):
                pe.wait_ge(s_on, 2 * b + 2)
                for t in range(T):
                    last = pe.transpose(MB[:, t * P:(t + 1) * P], TOK[:, b, t, :], ident[:, :])
                last.then_inc(s_ontp, 1)

            def y(b):
                if b == 0:
                    pe.wait_ge(s_w, 16 * 10)
                pe.wait_ge(s_ont, b + 1)
                for t in range(T):
                    last = pe.matmul(MB[:, t * D:(t + 1) * D], FT[:, b, t, :], Wo[:, :], start=True, stop=True)
                last.then_inc(s_yp, 1)

            def x2T(b):
                pe.wait_ge(s_ln[1], T * (b + 1))
                for t in range(T):
                    last = pe.transpose(MB[:, t * P:(t + 1) * P], TOK[:, b, t, :], ident[:, :])
                last.then_inc(s_x2tp, 1)

            def logits(b):
                pe.wait_ge(s_x2t, b + 1)
                for t in range(T):
                    last = pe.matmul(MB[:, t * NE:(t + 1) * NE], FT[:, b, t, :], WG[:, :], start=True, stop=True)
                last.then_inc(s_lgp, 1)

            def gT(b):
                pe.wait_ge(s_g, b + 1)
                for t in range(T):
                    last = pe.transpose(MB[0:NE, t * P:(t + 1) * P], G[:, b, t, :], ident[:, :])
                last.then_inc(s_gtp, 1)

            def bias(b):
                pe.wait_ge(s_gt, b + 1)
                for t in range(T):
                    last = pe.matmul(MB[:, t * DO:(t + 1) * DO], GT[:, b, t * P:(t + 1) * P], BE[:, :],
                                     start=True, stop=True)
                last.then_inc(s_bp, 1)

            def experts(b, k):
                t, half = k // 2, k % 2
                n = T * b + t
                if half == 0:
                    pe.wait_ge(s_r[1], min(b + 3, B))
                    if n >= 1:
                        pe.wait_ge(s_me[0], n)
                if half == 1:
                    if t == 0:
                        pe.wait_ge(s_xb, b + 1)
                    else:
                        pe.wait_ge(s_me[1], n)
                pe.matmul((ME, MB)[half][:, :], FT[:, b, t, :],
                          WE[:, 4 * half:4 * half + 4, :].rearrange("p e n -> p (e n)"),
                          start=True, stop=True).then_inc(s_mep[half], 1)

            xT(0)
            down(0)
            up(0, 0)
            up(0, 1)
            values(0)
            for u in range(-1, NU + 1):
                b = u // 2
                for n in range(NF if u < NU else LAG):
                    a = NF * u + n - LAG
                    if a >= 0:
                        att_fill(a // NF, a % NF)
                    if u + 1 < NU:
                        max_fill(u + 1, n)
                    if a >= 1 and FILLS[a % NF][0] != FILLS[(a - 1) % NF][0]:
                        pv((a - 1) // NF, I - FILLS[(a - 1) % NF][0])
                    if u % 2 == 0 and b + 1 < B:
                        if n == AT_XT:
                            xT(b + 1)
                        if n == AT_C:
                            down(b + 1)
                        if n == AT_Q:
                            up(b + 1, 0)
                        if n == AT_K:
                            up(b + 1, 1)
                        if n == AT_V:
                            values(b + 1)
                    if u % 2 == 0 and 1 <= b < B:
                        if n == AT_OT0:
                            oT(b - 1, 0)
                        if n == AT_OT1:
                            oT(b - 1, 1)
                        if n == AT_ONT:
                            onT(b - 1)
                        if n == AT_Y:
                            y(b - 1)
                        if n == AT_X2T:
                            x2T(b - 1)
                        if n == AT_LOG:
                            logits(b - 1)
                        if n == AT_GT:
                            gT(b - 1)
                        if n == AT_BIAS:
                            bias(b - 1)
                    if u % 2 == 1 and b >= 1 and n % 2 == AT_MOE % 2 and n // 2 < 2 * T:
                        experts(b - 1, n // 2)
                if u + 1 < NU:
                    max_turn(u + 1)
            pv(NU - 1, I - 1)
            b = B - 1
            oT(b, 0)
            oT(b, 1)
            onT(b)
            y(b)
            x2T(b)
            logits(b)
            gT(b)
            bias(b)
            for k in range(2 * T):
                experts(b, k)

        @block.scalar
        def _(act):
            act.dma_start(Wo[:, :], W_o).then_inc(s_w, 16)
            act.dma_start(WE[:, :, :], We.rearrange("e d o -> d e o")).then_inc(s_w, 16)
            act.dma_start(BE[:, :], be).then_inc(s_w, 16)
            act.dma_start(WG[:, :], Wg).then_inc(s_w, 16)
            act.dma_start(BG[:, :], bg.partition_broadcast(P)).then_inc(s_w, 16)

            def copy_xT(b):
                act.wait_ge(s_xtp, b + 1)
                act.copy(FT[:, b, :, :].rearrange("p t n -> p (t n)"), MA[:, :]).then_inc(s_xt, 1)

            def copy_c(b):
                act.wait_ge(s_cp, b + 1)
                act.copy(CT[:, b, :], MA[0:2 * C, :]).then_inc(s_c, 1)

            def part1(b, o):
                act.wait_ge(s_pp[o], b + 1)
                if b >= 2:
                    act.wait_ge(s_qs[b % 2], stacked(b - 2))
                act.copy(PT1[:, b % 2, o, :], (MA, ME)[o][:, :]).then_inc(s_p1[o], 1)

            def copy_v(b):
                act.wait_ge(s_vp, b + 1)
                act.wait_ge(s_vone, 2)
                if b >= 2:
                    act.wait_ge(s_pv, I * 2 * (b - 1))
                for s in range(2):
                    act.copy(VB[SUB * s:SUB * s + SUB, b % 2, :, :, DK * s:DK * s + DK],
                             MA[SUB * s:SUB * s + SUB, :].rearrange("k (i p e) -> k i p e", i=I, e=DK)
                             ).then_inc(s_v, 1)

            def shift_high(u):
                F = NMF * u + NF
                act.wait_ge(s_smf, F + 1)
                if u >= 2:
                    act.wait_ge(s_sh[u % 2], 64 * (u // 2))
                act.mul(SH[:, u % 2, 0, :], SM[F % 2][0:4 * I, 0:P], -1.0).then_inc(s_hi, 1)

            def exp(u, n):
                F = NF * u + n
                c, j0, m = FILLS[n]
                i = I - c
                act.wait_ge(s_saf, F + 1)
                if I * u + i >= 2:
                    act.wait_ge(s_pv, I * u + i - 1)
                act.activation(PR[:, i % 2, j0:j0 + m, 0:SUB * c],
                               SA[F % 2][:, 0:m * SUB * c].rearrange("p (j w) -> p j w", j=m),
                               ACT.Exp, scale=SCALE).then_inc(s_exp, 1)

            def copy_pv(u):
                act.wait_ge(s_pv, I * (u + 1))
                act.copy(OT[:, u // 2, u % 2, :], PV[:, :]).then_inc(s_ot, 1)

            def copy_onT(b):
                act.wait_ge(s_ontp, b + 1)
                act.copy(FT[:, b, :, :].rearrange("p t n -> p (t n)"), MB[:, :]).then_inc(s_ont, 1)

            def copy_x2T(b):
                act.wait_ge(s_x2tp, b + 1)
                act.copy(FT[:, b, :, :].rearrange("p t n -> p (t n)"), MB[:, :]).then_inc(s_x2t, 1)

            def top_exp(b):
                act.wait_ge(s_df, b + 1)
                act.activation(E1[:, b, :], DF[:, b, :], ACT.Exp).then_inc(s_e1, 1)

            def copy_gT(b):
                act.wait_ge(s_gtp, b + 1)
                act.copy(GT[:, b, :], MB[0:NE, :]).then_inc(s_gt, 1)

            def weigh_hi(b, t):
                n = T * b + t
                act.wait_ge(s_mep[1], n + 1)
                act.wait_ge(s_g, b + 1)
                if n >= 2:
                    act.wait_ge(s_o, n - 1)
                for e in range(4):
                    last = act.activation(PROD[:, n % 2, 4 + e, :], MB[:, e * DO:(e + 1) * DO], ACT.Copy,
                                          scale=G[:, b, t, 4 + e:5 + e])
                last.then_inc(s_me[1], 1)

            act.wait_ge(s_w, 16 * 10)
            act.copy(WP[:, :].rearrange("k (e s p) -> k p s e", s=2, p=NP),
                     Wu[:, 0, :].rearrange("k (p s e) -> k p s e", s=2, e=DK)).then_inc(s_wp, 1)
            copy_xT(0)
            copy_c(0)
            part1(0, 0)
            part1(0, 1)
            copy_v(0)
            for u in range(-1, NU + 1):
                b = u // 2
                for n in range(NF if u < NU else LAG):
                    a = NF * u + n - LAG
                    if a >= 0:
                        exp(a // NF, a % NF)
                    if a >= NF and a % NF == 1:
                        copy_pv(a // NF - 1)
                    if u % 2 == 0 and b + 1 < B:
                        if n == AT_XT:
                            copy_xT(b + 1)
                        if n == AT_C:
                            copy_c(b + 1)
                        if n == AT_Q:
                            part1(b + 1, 0)
                        if n == AT_K:
                            part1(b + 1, 1)
                        if n == AT_V:
                            copy_v(b + 1)
                    if u % 2 == 0 and 1 <= b < B:
                        if n == AT_ONT:
                            copy_onT(b - 1)
                        if n == AT_X2T:
                            copy_x2T(b - 1)
                        if n == AT_LOG + 1:
                            top_exp(b - 1)
                        if n == AT_GT:
                            copy_gT(b - 1)
                    if u % 2 == 1 and b >= 1 and n % 4 == 3 and n // 4 < T:
                        weigh_hi(b - 1, n // 4)
                if u + 1 < NU:
                    shift_high(u + 1)
            copy_pv(NU - 1)
            b = B - 1
            copy_onT(b)
            copy_x2T(b)
            top_exp(b)
            copy_gT(b)
            for t in range(T):
                weigh_hi(b, t)

        @block.vector
        def _(dve):
            def norm(k, b):
                for t in range(T):
                    dve.bn_stats(ST6[:, k, b, t, :], X[:, b, t, :]).then_inc(s_st[k], 1)
                dve.wait_ge(s_st[k], T * (b + 1))
                for t in range(T):
                    dve.bn_aggr(MV[:, k, b, t, :], ST6[:, k, b, t, :]).then_inc(s_mv[k], 1)
                dve.wait_ge(s_mv[k], T * (b + 1))
                dve.tensor_scalar(VE[:, k, b, :], MV[:, k, b, :, 1], EPS, None, ALU.add).then_inc(s_ve[k], 1)

            def norm_out(k, b):
                dve.wait_ge(s_rs[k], b + 1)
                for t in range(T):
                    dve.tensor_scalar(TOK[:, b, t, :], X[:, b, t, :], MV[:, k, b, t, 0:1],
                                      RS[:, k, b, t:t + 1], ALU.subtract, ALU.mult).then_inc(s_ln[k], 1)

            def zero_rows():
                for o in range(2):
                    dve.memset((QS, KS)[o][0:64, 0, :, :].rearrange("p h n -> p (h n)").bitcast(U32),
                               0).then_inc(s_zero[0], 1)

            def rest(b, o):
                dve.wait_ge(s_p1[o], b + 1)
                if b >= 2:
                    dve.wait_ge(s_qs[b % 2], stacked(b - 2))
                dve.tensor_tensor(RES[:, b % 2, o, :], (MA, ME)[o][:, :], PT1[:, b % 2, o, :],
                                  ALU.subtract).then_inc(s_r[o], 1)
                dve.wait_ge(s_r[o], b + 1)
                dve.tensor_copy(PT2[:, b % 2, o, :], RES[:, b % 2, o, :]).then_inc(s_p2[o], 1)

            def maxima(u, n):
                F = NMF * u + n
                c, j0, m = FILLS[n]
                dve.wait_ge(s_smf, F + 1)
                if n == 0 and u >= 2:
                    dve.wait_ge(s_smf, NMF * (u - 1))
                dve.tensor_reduce(MX[:, u % 2, j0:j0 + m, c - 1],
                                  SM[F % 2][:, 0:m * SUB * c].rearrange("p (j w) -> p j w", j=m),
                                  AX.X, ALU.max).then_inc(s_smr, 1)

            def shift_low(u):
                F = NMF * u + NF
                dve.wait_ge(s_hi, u + 1)
                dve.scalar_tensor_tensor(out=SH[:, u % 2, 1, :], in0=SM[F % 2][0:4 * I, 0:P], scalar=-1.0,
                                         in1=SH[:, u % 2, 0, :], op0=ALU.mult, op1=ALU.subtract
                                         ).then_inc(s_smr, 1)

            def normalise(b, half):
                k = 2 * b + half
                dve.wait_ge(s_otp, k + 1)
                o = MB[:, :].rearrange("p (a c) -> p a c", c=32)
                dve.reciprocal(RL[:, b, half, :, :], o[:, :, 2 * DK:2 * DK + 2]).then_inc(s_rl, 1)
                dve.wait_ge(s_rl, k + 1)
                dve.tensor_tensor(
                    TOK[:, b, 2 * half:2 * half + 2, :].rearrange("p t (a s e) -> p (t a) s e", s=2, e=DK),
                    o[:, :, 0:2 * DK].rearrange("p a (s e) -> p a s e", s=2),
                    RL[:, b, half, :, :].unsqueeze(3).to_broadcast([P, 16, 2, DK]), ALU.mult).then_inc(s_on, 1)

            def residual(b):
                dve.wait_ge(s_yp, b + 1)
                xb = X[:, b, :, :].rearrange("p t d -> p (t d)")
                dve.tensor_tensor(xb, MB[:, :], xb, ALU.add).then_inc(s_x1, 1)
                dve.wait_ge(s_x1, b + 1)

            def router(b):
                if b == 0:
                    dve.wait_ge(s_w, 16 * 10)
                dve.wait_ge(s_lgp, b + 1)
                dve.tensor_tensor(LG[:, b, :, :], MB[:, 0:T * NE].rearrange("p (t e) -> p t e", t=T),
                                  BG[:, :].unsqueeze(1).to_broadcast([P, T, NE]), ALU.add).then_inc(s_lg, 1)
                dve.wait_ge(s_lg, b + 1)
                for t in range(T):
                    dve.max(TOP[:, b, t, :], LG[:, b, t, :]).then_inc(s_top, 1)
                dve.wait_ge(s_top, T * (b + 1))
                dve.tensor_tensor(DF[:, b, :], TOP[:, b, :, 1], TOP[:, b, :, 0], ALU.subtract).then_inc(s_df, 1)
                for t in range(T):
                    dve.max_index(TIX[:, b, t, :], TOP[:, b, t, :], LG[:, b, t, :]).then_inc(s_tix, 1)
                dve.wait_ge(s_tix, T * (b + 1))
                dve.tensor_copy(TIF[:, b, :, :], TIX[:, b, :, 0:2]).then_inc(s_gate, 1)
                dve.wait_ge(s_const, 11)
                dve.wait_ge(s_gate, 8 * b + 1)
                for k in range(2):
                    dve.tensor_tensor(OH[:, b, k, :, :], iota8[:, :].unsqueeze(1).to_broadcast([P, T, NE]),
                                      TIF[:, b, :, k].unsqueeze(2).to_broadcast([P, T, NE]),
                                      ALU.is_equal).then_inc(s_gate, 1)

            def gates(b):
                dve.wait_ge(s_e1, b + 1)
                dve.tensor_scalar(DEN[:, b, :], E1[:, b, :], 1.0, None, ALU.add).then_inc(s_gate, 1)
                dve.wait_ge(s_gate, 8 * b + 4)
                dve.reciprocal(G12[:, b, 0, :], DEN[:, b, :]).then_inc(s_gate, 1)
                dve.wait_ge(s_gate, 8 * b + 5)
                dve.tensor_tensor(G12[:, b, 1, :], E1[:, b, :], G12[:, b, 0, :], ALU.mult).then_inc(s_gate, 1)
                dve.wait_ge(s_gate, 8 * b + 6)
                for k in range(2):
                    dve.tensor_tensor(GW[:, b, k, :, :], OH[:, b, k, :, :],
                                      G12[:, b, k, :].unsqueeze(2).to_broadcast([P, T, NE]),
                                      ALU.mult).then_inc(s_gate, 1)
                dve.wait_ge(s_gate, 8 * b + 8)
                dve.tensor_tensor(G[:, b, :, :], GW[:, b, 0, :, :], GW[:, b, 1, :, :], ALU.add).then_inc(s_g, 1)

            def add_bias(b):
                dve.wait_ge(s_bp, b + 1)
                xb = X[:, b, :, :].rearrange("p t d -> p (t d)")
                dve.tensor_tensor(xb, MB[:, :], xb, ALU.add).then_inc(s_xb, 1)

            def weigh_lo(b, t):
                n = T * b + t
                dve.wait_ge(s_mep[0], n + 1)
                dve.wait_ge(s_g, b + 1)
                if n >= 2:
                    dve.wait_ge(s_o, n - 1)
                dve.tensor_tensor(PROD[:, n % 2, 0:4, :], ME[:, :].rearrange("p (e o) -> p e o", e=4),
                                  G[:, b, t, 0:4].unsqueeze(2).to_broadcast([P, 4, DO]),
                                  ALU.mult).then_inc(s_me[0], 1)

            dve.wait_ge(s_x[0], 16)
            norm(0, 0)
            norm_out(0, 0)
            zero_rows()
            rest(0, 0)
            rest(0, 1)
            for u in range(-1, NU):
                b = u // 2
                for n in range(NF):
                    if u + 1 < NU:
                        maxima(u + 1, n)
                    if u % 2 == 0 and b + 1 < B:
                        if n == AT_Q + 1:
                            rest(b + 1, 0)
                        if n == AT_K + 1:
                            rest(b + 1, 1)
                    if u % 2 == 0 and 1 <= b < B:
                        if n == AT_OT0:
                            normalise(b - 1, 0)
                        if n == AT_OT1:
                            normalise(b - 1, 1)
                        if n == AT_Y:
                            residual(b - 1)
                            norm(1, b - 1)
                        if n == AT_Y + 2:
                            norm_out(1, b - 1)
                        if n == AT_LOG:
                            router(b - 1)
                        if n == AT_LOG + 2:
                            gates(b - 1)
                        if n == AT_BIAS:
                            add_bias(b - 1)
                    if u % 2 == 1 and b >= 1 and n % 4 == 1 and n // 4 < T:
                        weigh_lo(b - 1, n // 4)
                    if u % 2 == 1 and b + 2 < B:
                        if n == AT_LN1 - 2:
                            dve.wait_ge(s_x[b + 2], 16)
                            norm(0, b + 2)
                        if n == AT_LN1:
                            norm_out(0, b + 2)
                if u + 1 < NU:
                    shift_low(u + 1)
            b = B - 1
            normalise(b, 0)
            normalise(b, 1)
            residual(b)
            norm(1, b)
            norm_out(1, b)
            router(b)
            gates(b)
            add_bias(b)
            for t in range(T):
                weigh_lo(b, t)


_INS = ["L0_attn_x", "L0_attn_W_dq", "L0_attn_W_uq", "L0_attn_W_dkv", "L0_attn_W_uk", "L0_attn_W_uv",
        "L0_attn_W_o", "L0_ffn_We", "L0_ffn_be", "L0_ffn_Wg", "L0_ffn_bg"]


def kernel(**inputs):
    import numpy as _np
    import concourse.bacc as _bacc
    from concourse import mybir as _mybir
    from concourse.bass_utils import run_bass_kernel_spmd as _run

    nc = _bacc.Bacc("TRN2", target_bir_lowering=False, num_devices=1)
    arrays, args = {}, []
    for name in _INS:
        a = _np.ascontiguousarray(inputs[name])
        arrays[f"in_{name}_dram"] = a
        args.append(nc.dram_tensor(f"in_{name}_dram", a.shape, _mybir.dt.from_np(a.dtype), kind="ExternalInput").ap())
    shape = inputs["L0_attn_x"].shape
    args.append(nc.dram_tensor("out_0_dram", shape, _mybir.dt.float32, kind="ExternalOutput").ap())
    build(nc, *args)
    r = _run(nc, [arrays], core_ids=[0])
    return r.results[0]["out_0_dram"]
```

```python
from contextlib import ExitStack

import concourse.bass as bass
from concourse import mybir

F32 = mybir.dt.float32
BF16 = mybir.dt.bfloat16
U32 = mybir.dt.uint32
ALU = mybir.AluOpType
ACT = mybir.ActivationFunctionType
AX = mybir.AxisListType

P = 128
SUB = 64
EPS = 1e-5
BIG = 1e30
PARTS = ((0, 0), (0, 1), (1, 0), (0, 2), (2, 0), (1, 1))

LAG = 5
NSM = 3

AT_MOE, AT_LN1, AT_XT, AT_C, AT_Q, AT_K = 0, 8, 14, 16, 18, 20
AT_OT0, AT_OT1, AT_ONT, AT_Y, AT_X2T, AT_LOG = 7, 8, 10, 12, 17, 19
AT_V = 10
AT_LN1OUT, AT_LN2OUT, AT_TOP, AT_GATE = 12, 15, 20, 21
BEHIND = 0


def fill_plan(SUBS, bank):
    plan = []
    for c in range(SUBS, 0, -1):
        m = min(4, bank // (SUB * c))
        m = 4 if m == 3 else m
        m = 2 if m == 2 else m
        for j in range(0, 4, m):
            plan.append((c, j, m))
    return plan


def build(nc, x, W_dq, W_uq, W_dkv, W_uk, W_uv, W_o, We, be, Wg, bg, out):
    B, S, D = x.shape
    C = W_dq.shape[1]
    NE, _, DO = We.shape
    H = 16
    DK = D // H
    T = S // P
    I = S // SUB
    NP = H // 2
    NU = 2 * B
    SCALE = float(DK) ** -0.5
    FILLS = fill_plan(I, S)
    NF = len(FILLS)
    NMF = NF + 1
    NDMA = len(PARTS) * 2 + 1

    with ExitStack() as ctx:
        def sb(name, shape, dt):
            return ctx.enter_context(nc.sbuf_tensor(name, shape, dt))

        def pb(name):
            return ctx.enter_context(nc.psum_tensor(name, [P, 512], F32))

        def sem(name):
            return ctx.enter_context(nc.semaphore(name))

        QS = sb("QS", [P, 2, H, S], BF16)
        KS = sb("KS", [P, 2, H, S], BF16)
        VB = sb("VB", [P, 2, I, NP, 32], F32)
        PR = sb("PR", [P, 2, 4, S], F32)
        X = sb("X", [P, B, T, D], F32)
        TOK = sb("TOK", [P, B, T, D], F32)
        FT = sb("FT", [P, B, T, P], F32)
        CT = sb("CT", [2 * C, B, S], F32)
        OT = sb("OT", [P, 2, 2, S], F32)
        PT1 = sb("PT1", [P, 2, 2, S], BF16)
        PT2 = sb("PT2", [P, 2, 2, S], BF16)
        PT3 = sb("PT3", [P, 2, 2, S], BF16)
        RES = sb("RES", [P, 2, 2, S], F32)
        MX = sb("MX", [P, 2, 4, I], F32)
        SH = sb("SH", [4 * I, 2, 2, P], BF16)
        Wd = sb("Wd", [P, 2 * C], F32)
        Wu = sb("Wu", [2 * C, 2, P], F32)
        WP = sb("WP", [2 * C, P], F32)
        Wo = sb("Wo", [P, D], F32)
        WE = sb("WE", [P, NE, DO], F32)
        BE = sb("BE", [1, NE * DO], F32)
        BR = sb("BR", [1, NE * DO], F32)
        BP = sb("BP", [1, 3, NE * DO], BF16)
        BEP = sb("BEP", [P, NE * DO], BF16)
        WG = sb("WG", [P, NE], F32)
        BG = sb("BG", [P, NE], F32)
        ident = sb("ident", [P, P], F32)
        identb = sb("identb", [P, P], BF16)
        MSK = sb("MSK", [P, 2, SUB], BF16)
        ZR = sb("ZR", [P, S], BF16)
        ON = sb("ON", [P, S], BF16)
        mhalf = sb("mhalf", [P, T], F32)
        iota8 = sb("iota8", [P, NE], F32)
        ST6 = sb("ST6", [P, 2, B, T, 6], F32)
        MV = sb("MV", [P, 2, B, T, 2], F32)
        VE = sb("VE", [P, 2, B, T], F32)
        RS = sb("RS", [P, 2, B, T], F32)
        RL = sb("RL", [P, B, 2, 16, 2], F32)
        LG = sb("LG", [P, B, T, NE], F32)
        TOP = sb("TOP", [P, B, T, 8], F32)
        TIX = sb("TIX", [P, B, T, 8], U32)
        TIF = sb("TIF", [P, B, T, 2], F32)
        DF = sb("DF", [P, B, T], F32)
        E1 = sb("E1", [P, B, T], F32)
        DEN = sb("DEN", [P, B, T], F32)
        G12 = sb("G12", [P, B, 2, T], F32)
        OH = sb("OH", [P, B, 2, T, NE], F32)
        GW = sb("GW", [P, B, 2, T, NE], F32)
        G = sb("G", [P, B, T, NE], F32)
        PROD = sb("PROD", [P, 2, NE, DO], F32)
        SUM4 = sb("SUM4", [P, 4, DO], F32)
        SUM2 = sb("SUM2", [P, 2, DO], F32)
        SUM1 = sb("SUM1", [P, DO], F32)

        SM = [pb(f"SM{n}") for n in range(NSM)]
        SA = [pb("SA0"), pb("SA1")]
        PV = pb("PV")
        MA = pb("MA")
        MB = pb("MB")

        s_w = sem("weights_in")
        s_wp = sem("up_weights_permuted")
        s_x = [sem(f"x_in{b}") for b in range(B)]
        s_const = sem("constants_made")
        s_on1 = sem("one_rows_made")
        s_vz = sem("value_zeros_made")
        s_vone = sem("value_ones_made")
        s_pad = sem("pad_rows_in")
        s_zero = [sem("zero_rows_made0"), sem("zero_rows_made1")]
        s_st = [sem("ln1_stats"), sem("ln2_stats")]
        s_mv = [sem("ln1_meanvar"), sem("ln2_meanvar")]
        s_ve = [sem("ln1_var_eps"), sem("ln2_var_eps")]
        s_rs = [sem("ln1_rstd"), sem("ln2_rstd")]
        s_ln = [sem("ln1_out"), sem("ln2_out")]
        s_xtp = sem("xT_in_psum")
        s_xt = sem("xT_copied")
        s_cp = sem("c_in_psum")
        s_c = sem("c_copied")
        s_pp = [sem("q_in_psum"), sem("k_in_psum")]
        s_p1 = [sem("q_part1"), sem("k_part1")]
        s_r = [sem("q_rest"), sem("k_rest")]
        s_p2 = [sem("q_part2"), sem("k_part2")]
        s_p3 = [sem("q_part3"), sem("k_part3")]
        s_vp = sem("v_in_psum")
        s_v = sem("v_copied")
        s_qs = [sem("stacked_in0"), sem("stacked_in1")]
        s_smf = sem("max_bank_filled")
        s_smr = sem("max_bank_read")
        s_hi = sem("shift_high")
        s_sh = [sem("shift_rows_in0"), sem("shift_rows_in1")]
        s_saf = sem("att_bank_filled")
        s_exp = sem("exp_done")
        s_pv = sem("pv_done")
        s_ot = sem("pv_copied")
        s_otp = sem("oT_in_psum")
        s_rl = sem("recip_done")
        s_on = sem("o_normalised")
        s_ontp = sem("onT_in_psum")
        s_ont = sem("onT_copied")
        s_yp = sem("y_in_psum")
        s_x1 = sem("x1_done")
        s_x2tp = sem("x2T_in_psum")
        s_x2t = sem("x2T_copied")
        s_lgp = sem("logits_in_psum")
        s_lg = sem("logits_done")
        s_top = sem("top8_done")
        s_tix = sem("top8_index_done")
        s_df = sem("top_difference")
        s_e1 = sem("top_exp")
        s_gate = sem("gate_steps")
        s_g = sem("gates_done")
        s_b = sem("bias_steps")
        s_bz = sem("bias_zero_rows_made")
        s_bin = sem("bias_rows_in")
        s_mep = [sem("experts_lo_in_psum"), sem("experts_hi_in_psum")]
        s_me = [sem("experts_lo_weighted"), sem("experts_hi_weighted")]
        s_sum = sem("expert_sums")
        s_o = sem("tile_out")
        s_store = sem("stored")

        block = ctx.enter_context(nc.Block())

        def qk_bank(b, o):
            return MB if (b, o) == (0, 1) else MA

        def expert_bank(b, t, half):
            if b < B - 1:
                return (MA, MB)[half]
            return (SM + SA + [PV, MA, MB])[2 * t + half]

        def stacked(b):
            return 16 * NDMA * (b // 2 + 1)

        @block.sync
        def _(sp):
            for b in range(B):
                sp.dma_start(X[:, b, :, :], x[b].rearrange("(t p) d -> p t d", p=P)).then_inc(s_x[b], 16)
                if b == 0:
                    sp.dma_start(Wd[:, 0:C], W_dq).then_inc(s_w, 16)
                    sp.dma_start(Wd[:, C:2 * C], W_dkv).then_inc(s_w, 16)
                    sp.dma_start(Wu[0:C, 0, :], W_uq).then_inc(s_w, 16)
                    sp.dma_start(Wu[C:2 * C, 0, :], W_uk).then_inc(s_w, 16)
                    sp.dma_start(Wu[C:2 * C, 1, :], W_uv).then_inc(s_w, 16)
            sp.wait_ge(s_on1, 1)
            for par in range(2):
                sp.dma_start(QS[120:128, par, :, :], ZR[:, :]).then_inc(s_pad, 16)
                sp.dma_start(KS[112:120, par, :, :], ON[:, :]).then_inc(s_pad, 16)
                sp.dma_start(KS[120:128, par, :, :], ZR[:, :]).then_inc(s_pad, 16)

            def zero_rows(par):
                for o in range(2):
                    sp.dma_start((QS, KS)[o][0:64, par, :, :],
                                 ZR[0:64, :].unsqueeze(1).to_broadcast([64, H, S])).then_inc(s_zero[par], 16)

            def stack(b):
                if b >= 2:
                    sp.wait_ge(s_saf, NF * 2 * (b - 1))
                sp.dma_start(QS[112:120, b % 2, :, :], ZR[:, :]).then_inc(s_qs[b % 2], 16)
                for level in range(3):
                    for o in range(2):
                        sp.wait_ge((s_p1, s_p2, s_p3)[level][o], b + 1)
                        src = (PT1, PT2, PT3)[level][:, b % 2, o, :]
                        for n, pair in enumerate(PARTS):
                            if pair[o] == level:
                                r = 64 + 8 * n
                                sp.dma_start((QS, KS)[o][r:r + 8, b % 2, :, :], src).then_inc(s_qs[b % 2], 16)

            def shift_rows(u):
                sp.wait_ge(s_smr, NMF * (u + 1))
                g = u % 2
                for part in range(2):
                    for s in range(2):
                        h = NP * s + 4 * g
                        sp.dma_start(QS[112 + part:113 + part, (u // 2) % 2, h:h + 4, :], SH[:, u % 2, part, SUB * s:SUB * s + SUB]).then_inc(s_sh[u % 2], 16)

            def store(b):
                for t in range(T):
                    sp.wait_ge(s_o, T * b + t + 1)
                    sp.dma_start(out[b, t * P:(t + 1) * P, :], TOK[:, b, t, :]).then_inc(s_store, 16)

            stack(0)
            zero_rows(1)
            sp.wait_ge(s_bz, 1)
            sp.wait_ge(s_b, 5)
            for n in range(3):
                sp.dma_start(BEP[n:n + 1, :], BP[0:1, n, :]).then_inc(s_bin, 16)
            for u in range(-1, NU):
                b = u // 2
                if u % 2 == 1 and b >= 1:
                    store(b - 1)
                if u + 1 < NU:
                    shift_rows(u + 1)
                if u % 2 == 1 and b + 2 < B:
                    stack(b + 2)
            store(B - 1)
            sp.wait_ge(s_store, 16 * B * T)

        @block.gpsimd
        def _(pool):
            pool.memset(ZR[:, :], 0.0).then_inc(s_const, 1)
            pool.memset(ON[:, :], 0.0).then_inc(s_const, 1)
            pool.memset(ident[:, :], 0.0).then_inc(s_const, 1)
            pool.memset(mhalf[:, :], -0.5).then_inc(s_const, 1)
            pool.wait_ge(s_const, 4)
            pool.memset(ON[0:32, :], 1.0).then_inc(s_on1, 1)
            pool.wait_ge(s_on1, 1)
            pool.affine_select(out=ident[:, :], in_=ident[:, :], compare_op=ALU.not_equal, fill=1.0, base=0,
                               pattern=[[-1, P]], channel_multiplier=1).then_inc(s_const, 1)
            pool.affine_select(out=identb[:, :], in_=ZR[:, 0:P], compare_op=ALU.not_equal, fill=1.0, base=0,
                               pattern=[[-1, P]], channel_multiplier=1).then_inc(s_const, 1)
            for o, sign in ((0, 1), (1, -1)):
                pool.affine_select(out=MSK[:, o, :], in_=ZR[:, 0:SUB], compare_op=ALU.is_ge, fill=-BIG,
                                   base=-SUB * sign, pattern=[[-sign, SUB]],
                                   channel_multiplier=sign).then_inc(s_const, 1)
            pool.wait_ge(s_const, 8)
            for o, sign in ((0, 1), (1, -1)):
                pool.affine_select(out=MSK[0:SUB, o, :], in_=ZR[0:SUB, 0:SUB], compare_op=ALU.is_ge, fill=-BIG,
                                   base=0, pattern=[[-sign, SUB]], channel_multiplier=sign).then_inc(s_const, 1)
            pool.wait_ge(s_const, 10)
            pool.iota(iota8[:, :], pattern=[[1, NE]], base=0, channel_multiplier=0,
                      allow_small_or_imprecise_dtypes=True).then_inc(s_const, 1)

            def rstd(k, b):
                pool.wait_ge(s_ve[k], b + 1)
                pool.tensor_tensor(RS[:, k, b, :], VE[:, k, b, :], mhalf[:, :], ALU.pow).then_inc(s_rs[k], 1)

            def third_parts(b):
                for o in range(2):
                    pool.wait_ge(s_p2[o], b + 1)
                    if b >= 2:
                        pool.wait_ge(s_qs[b % 2], stacked(b - 2))
                    pool.tensor_tensor(PT3[:, b % 2, o, :], RES[:, b % 2, o, :], PT2[:, b % 2, o, :],
                                       ALU.subtract).then_inc(s_p3[o], 1)

            def expert_sums(b, t):
                n = T * b + t
                pr = PROD[:, n % 2, :, :]
                pool.wait_ge(s_me[0], n + 1)
                pool.wait_ge(s_me[1], n + 1)
                pool.tensor_tensor(SUM4[:, :, :], pr[:, 0:4, :], pr[:, 4:8, :], ALU.add).then_inc(s_sum, 1)
                pool.wait_ge(s_sum, 3 * n + 1)
                pool.tensor_tensor(SUM2[:, :, :], SUM4[:, 0:2, :], SUM4[:, 2:4, :], ALU.add).then_inc(s_sum, 1)
                pool.wait_ge(s_sum, 3 * n + 2)
                pool.tensor_tensor(SUM1[:, :], SUM2[:, 0, :], SUM2[:, 1, :], ALU.add).then_inc(s_sum, 1)
                pool.wait_ge(s_sum, 3 * n + 3)
                pool.wait_ge(s_x1, b + 1)
                pool.tensor_tensor(TOK[:, b, t, :], SUM1[:, :], X[:, b, t, :], ALU.add).then_inc(s_o, 1)
                pool.wait_ge(s_o, n + 1)

            rstd(0, 0)
            pool.memset(VB[:, :, :, :, :], 0.0).then_inc(s_vz, 1)
            pool.wait_ge(s_vz, 1)
            pool.memset(VB[0:SUB, :, :, :, 2 * DK:2 * DK + 1], 1.0).then_inc(s_vone, 1)
            pool.wait_ge(s_vone, 1)
            pool.memset(VB[SUB:P, :, :, :, 2 * DK + 1:2 * DK + 2], 1.0).then_inc(s_vone, 1)
            pool.wait_ge(s_vone, 2)
            third_parts(0)
            pool.memset(BEP[:, :], 0.0).then_inc(s_bz, 1)
            for u in range(-1, NU):
                b = u // 2
                if u % 2 == 0:
                    if b >= 1:
                        rstd(1, b - 1)
                else:
                    for t in range(T):
                        if b + 2 < B and t == 2:
                            rstd(0, b + 2)
                        if b >= 1:
                            expert_sums(b - 1, t)
                    if b + 2 < B:
                        third_parts(b + 2)
            rstd(1, B - 1)
            for t in range(T):
                expert_sums(B - 1, t)

        @block.tensor
        def _(pe):
            def xT(b):
                pe.wait_ge(s_const, 5)
                pe.wait_ge(s_ln[0], T * (b + 1))
                if b >= 1:
                    pe.wait_ge(s_v, 2 * b)
                if b >= 3:
                    pe.wait_ge(s_me[0], T * (b - 2))
                for t in range(T):
                    last = pe.transpose(MA[:, t * P:(t + 1) * P], TOK[:, b, t, :], ident[:, :])
                last.then_inc(s_xtp, 1)

            def down(b):
                pe.wait_ge(s_w, 16 * 10)
                pe.wait_ge(s_xt, b + 1)
                pe.matmul(MA[0:2 * C, :], Wd[:, :], FT[:, b, :, :].rearrange("p t n -> p (t n)"),
                          start=True, stop=True).then_inc(s_cp, 1)

            def up(b, o):
                pe.wait_ge(s_c, b + 1)
                if o == 1 and b >= 1:
                    pe.wait_ge(s_r[0], b + 1)
                pe.wait_ge(s_wp, 1)
                pe.matmul(qk_bank(b, o)[:, :], WP[C * o:C * o + C, :], CT[C * o:C * o + C, b, :], start=True, stop=True).then_inc(s_pp[o], 1)

            def values(b):
                pe.wait_ge(s_r[0 if b == 0 else 1], b + 1)
                w = Wu[C:2 * C, 1, :].rearrange("k (p s e) -> k s p e", s=2, e=DK)
                for i in range(I):
                    for s in range(2):
                        last = pe.matmul(MA[SUB * s:SUB * s + SUB, SUB * i:SUB * i + SUB],
                                         CT[C:2 * C, b, SUB * i:SUB * i + SUB], w[:, s], start=True, stop=True)
                last.then_inc(s_vp, 1)

            def max_fill(u, n):
                b, g, F = u // 2, u % 2, NMF * u + n
                if n == 0 and g == 0:
                    pe.wait_ge(s_qs[b % 2], stacked(b))
                    pe.wait_ge(s_zero[b % 2], 32 if b % 2 else 2)
                    pe.wait_ge(s_const, 10)
                    pe.wait_ge(s_pad, 96)
                if F >= NSM:
                    pe.wait_ge(s_smr, F - NSM + 1)
                c, j0, m = FILLS[n]
                i, bank = c - 1, SM[F % NSM]
                for j in range(m):
                    for s in range(2):
                        h = NP * s + 4 * g + j0 + j
                        pe.matmul(bank[SUB * s:SUB * s + SUB, SUB * c * j:SUB * c * (j + 1)],
                                  QS[:, b % 2, h, SUB * i:SUB * c], KS[:, b % 2, h, 0:SUB * c],
                                  start=(j == 0), stop=False, skip_group_check=True)
                last = pe.matmul(bank[:, 0:m * SUB * c].rearrange("p (j w) -> p j w", j=m)[:, :, SUB * i:SUB * c],
                                 identb[:, :], MSK[:, 0, :].unsqueeze(1).to_broadcast([P, m, SUB]),
                                 start=False, stop=True, skip_group_check=True)
                last.then_inc(s_smf, 1)

            def max_turn(u):
                F = NMF * u + NF
                pe.wait_ge(s_smr, F)
                pe.transpose(SM[F % NSM][0:4 * I, 0:P], MX[:, u % 2, :, :].rearrange("p j i -> p (j i)"),
                             ident[:, :]).then_inc(s_smf, 1)

            def att_fill(u, n):
                b, g, F = u // 2, u % 2, NF * u + n
                if n == 0:
                    pe.wait_ge(s_sh[u % 2], 64 * (u // 2 + 1))
                if F >= 2:
                    pe.wait_ge(s_exp, F - 1)
                c, j0, m = FILLS[n]
                i, bank = I - c, SA[F % 2]
                for j in range(m):
                    for s in range(2):
                        h = NP * s + 4 * g + j0 + j
                        pe.matmul(bank[SUB * s:SUB * s + SUB, SUB * c * j:SUB * c * (j + 1)],
                                  KS[:, b % 2, h, SUB * i:SUB * i + SUB], QS[:, b % 2, h, SUB * i:S],
                                  start=(j == 0), stop=False, skip_group_check=True)
                last = pe.matmul(bank[:, 0:m * SUB * c].rearrange("p (j w) -> p j w", j=m)[:, :, 0:SUB],
                                 identb[:, :], MSK[:, 1, :].unsqueeze(1).to_broadcast([P, m, SUB]),
                                 start=False, stop=True, skip_group_check=True)
                last.then_inc(s_saf, 1)

            def pv(u, i):
                b, g = u // 2, u % 2
                done = sum(1 for c, _, _ in FILLS if I - c <= i)
                pe.wait_ge(s_exp, NF * u + done)
                if i == 0:
                    pe.wait_ge(s_v, 2 * (b + 1))
                    pe.wait_ge(s_vone, 2)
                    if u >= 1:
                        pe.wait_ge(s_ot, u)
                for j in range(4):
                    last = pe.matmul(PV[32 * j:32 * j + 32, SUB * i:S], VB[:, b % 2, i, 4 * g + j, :],
                                     PR[:, i % 2, j, 0:S - SUB * i], start=(i == 0), stop=(i == I - 1))
                last.then_inc(s_pv, 1)

            def oT(b, half):
                pe.wait_ge(s_ot, 2 * b + 2)
                if half:
                    pe.wait_ge(s_on, 2 * b + 1)
                elif b >= 1:
                    pe.wait_ge(s_me[1], T * b)
                for tt in range(2):
                    t = 2 * half + tt
                    for g in range(2):
                        last = pe.transpose(MB[:, (2 * tt + g) * P:(2 * tt + g + 1) * P],
                                            OT[:, b % 2, g, t * P:(t + 1) * P], ident[:, :])
                last.then_inc(s_otp, 1)

            def onT(b):
                pe.wait_ge(s_on, 2 * b + 2)
                for t in range(T):
                    last = pe.transpose(MB[:, t * P:(t + 1) * P], TOK[:, b, t, :], ident[:, :])
                last.then_inc(s_ontp, 1)

            def y(b):
                if b == 0:
                    pe.wait_ge(s_w, 16 * 10)
                pe.wait_ge(s_ont, b + 1)
                for t in range(T):
                    last = pe.matmul(MB[:, t * D:(t + 1) * D], FT[:, b, t, :], Wo[:, :], start=True, stop=True)
                last.then_inc(s_yp, 1)

            def x2T(b):
                pe.wait_ge(s_ln[1], T * (b + 1))
                for t in range(T):
                    last = pe.transpose(MB[:, t * P:(t + 1) * P], TOK[:, b, t, :], ident[:, :])
                last.then_inc(s_x2tp, 1)

            def logits(b):
                pe.wait_ge(s_x2t, b + 1)
                for t in range(T):
                    last = pe.matmul(MB[:, t * NE:(t + 1) * NE], FT[:, b, t, :], WG[:, :], start=True, stop=True)
                last.then_inc(s_lgp, 1)

            def experts(b, k):
                t, half = k // 2, k % 2
                n = T * b + t
                if b == 0 and k == 0:
                    pe.wait_ge(s_bin, 48)
                if b < B - 1 and t == 0:
                    if half == 0 and b + 2 < B:
                        pe.wait_ge(s_v, 2 * (b + 3))
                    if half == 1:
                        pe.wait_ge(s_lg, b + 1)
                if b < B - 1 and n >= 1:
                    pe.wait_ge(s_me[half], n)
                if b == B - 1 and k == 0:
                    pe.wait_ge(s_smr, NMF * NU)
                    pe.wait_ge(s_exp, NF * NU)
                    pe.wait_ge(s_ot, NU)
                    pe.wait_ge(s_me[0], n)
                if b == B - 1 and k == 7:
                    pe.wait_ge(s_lg, b + 1)
                bank = expert_bank(b, t, half)
                cols = slice(4 * DO * half, 4 * DO * (half + 1))
                pe.matmul(bank[:, :], FT[:, b, t, :], WE[:, :, :].rearrange("p e n -> p (e n)")[:, cols],
                          start=True, stop=False)
                pe.matmul(bank[:, :], ON[:, 0:P], BEP[:, cols], start=False, stop=True).then_inc(s_mep[half], 1)

            xT(0)
            down(0)
            up(0, 0)
            up(0, 1)
            values(0)
            for u in range(-1, NU + 1):
                b = u // 2
                for n in range(NF if u < NU else LAG):
                    a = NF * u + n - LAG
                    if a >= 0:
                        att_fill(a // NF, a % NF)
                    if u + 1 < NU:
                        max_fill(u + 1, n)
                    if a >= 1 and FILLS[a % NF][0] != FILLS[(a - 1) % NF][0]:
                        pv((a - 1) // NF, I - FILLS[(a - 1) % NF][0])
                    if u % 2 == 1 and 1 <= b < B and n % 2 == AT_MOE % 2 and n // 2 < 2 * T:
                        experts(b - 1, n // 2)
                    if u % 2 == 1 and b + 2 < B:
                        if n == AT_XT:
                            xT(b + 2)
                        if n == AT_C:
                            down(b + 2)
                        if n == AT_Q:
                            up(b + 2, 0)
                        if n == AT_K:
                            up(b + 2, 1)
                    if u % 2 == 0 and b + 1 < B and n == AT_V:
                        values(b + 1)
                    if u % 2 == 0 and 1 <= b < B:
                        if n == AT_OT0:
                            oT(b - 1, 0)
                        if n == AT_OT1:
                            oT(b - 1, 1)
                        if n == AT_ONT:
                            onT(b - 1)
                        if n == AT_Y:
                            y(b - 1)
                        if n == AT_X2T:
                            x2T(b - 1)
                        if n == AT_LOG:
                            logits(b - 1)
                if u + 1 < NU:
                    max_turn(u + 1)
            pv(NU - 1, I - 1)
            b = B - 1
            oT(b, 0)
            oT(b, 1)
            onT(b)
            y(b)
            x2T(b)
            logits(b)
            for k in range(2 * T):
                experts(b, k)

        @block.scalar
        def _(act):
            act.dma_start(Wo[:, :], W_o).then_inc(s_w, 16)
            act.dma_start(WE[:, :, :], We.rearrange("e d o -> d e o")).then_inc(s_w, 16)
            act.dma_start(BE[:, :], be.rearrange("(a e) o -> a (e o)", a=1)).then_inc(s_w, 16)
            act.dma_start(WG[:, :], Wg).then_inc(s_w, 16)
            act.dma_start(BG[:, :], bg.partition_broadcast(P)).then_inc(s_w, 16)

            def copy_xT(b):
                act.wait_ge(s_xtp, b + 1)
                act.copy(FT[:, b, :, :].rearrange("p t n -> p (t n)"), MA[:, :]).then_inc(s_xt, 1)

            def copy_c(b):
                act.wait_ge(s_cp, b + 1)
                act.copy(CT[:, b, :], MA[0:2 * C, :]).then_inc(s_c, 1)

            def part1(b, o):
                act.wait_ge(s_pp[o], b + 1)
                if b >= 2:
                    act.wait_ge(s_qs[b % 2], stacked(b - 2))
                act.copy(PT1[:, b % 2, o, :], qk_bank(b, o)[:, :]).then_inc(s_p1[o], 1)

            def copy_v(b):
                act.wait_ge(s_vp, b + 1)
                act.wait_ge(s_vone, 2)
                if b >= 2:
                    act.wait_ge(s_pv, I * 2 * (b - 1))
                for s in range(2):
                    act.copy(VB[SUB * s:SUB * s + SUB, b % 2, :, :, DK * s:DK * s + DK],
                             MA[SUB * s:SUB * s + SUB, :].rearrange("k (i p e) -> k i p e", i=I, e=DK)
                             ).then_inc(s_v, 1)

            def shift_high(u):
                F = NMF * u + NF
                act.wait_ge(s_smf, F + 1)
                if u >= 2:
                    act.wait_ge(s_sh[u % 2], 64 * (u // 2))
                act.mul(SH[:, u % 2, 0, :], SM[F % NSM][0:4 * I, 0:P], -1.0).then_inc(s_hi, 1)

            def exp(u, n):
                F = NF * u + n
                c, j0, m = FILLS[n]
                i = I - c
                act.wait_ge(s_saf, F + 1)
                if I * u + i >= 2:
                    act.wait_ge(s_pv, I * u + i - 1)
                act.activation(PR[:, i % 2, j0:j0 + m, 0:SUB * c],
                               SA[F % 2][:, 0:m * SUB * c].rearrange("p (j w) -> p j w", j=m),
                               ACT.Exp, scale=SCALE).then_inc(s_exp, 1)

            def copy_pv(u):
                act.wait_ge(s_pv, I * (u + 1))
                if u >= 4:
                    act.wait_ge(s_otp, 2 * (u // 2 - 1))
                act.copy(OT[:, (u // 2) % 2, u % 2, :], PV[:, :]).then_inc(s_ot, 1)

            def copy_onT(b):
                act.wait_ge(s_ontp, b + 1)
                act.copy(FT[:, b, :, :].rearrange("p t n -> p (t n)"), MB[:, :]).then_inc(s_ont, 1)

            def copy_x2T(b):
                act.wait_ge(s_x2tp, b + 1)
                act.copy(FT[:, b, :, :].rearrange("p t n -> p (t n)"), MB[:, :]).then_inc(s_x2t, 1)

            def top_exp(b):
                act.wait_ge(s_df, b + 1)
                act.activation(E1[:, b, :], DF[:, b, :], ACT.Exp).then_inc(s_e1, 1)

            def weigh_hi(b, t):
                n = T * b + t
                act.wait_ge(s_mep[1], n + 1)
                act.wait_ge(s_g, b + 1)
                if n >= 2:
                    act.wait_ge(s_o, n - 1)
                for e in range(4):
                    last = act.activation(PROD[:, n % 2, 4 + e, :], expert_bank(b, t, 1)[:, e * DO:(e + 1) * DO], ACT.Copy,
                                          scale=G[:, b, t, 4 + e:5 + e])
                last.then_inc(s_me[1], 1)

            act.wait_ge(s_w, 16 * 10)
            act.copy(BP[:, 0, :], BE[:, :]).then_inc(s_b, 1)
            act.copy(WP[:, :].rearrange("k (e s p) -> k p s e", s=2, p=NP),
                     Wu[:, 0, :].rearrange("k (p s e) -> k p s e", s=2, e=DK)).then_inc(s_wp, 1)
            copy_xT(0)
            copy_c(0)
            part1(0, 0)
            part1(0, 1)
            copy_v(0)
            for u in range(-1, NU + 1):
                b = u // 2
                for n in range(NF if u < NU else LAG):
                    a = NF * u + n - LAG
                    if a >= 0:
                        exp(a // NF, a % NF)
                    if a >= NF and a % NF == 1:
                        copy_pv(a // NF - 1)
                    if u % 2 == 1 and b + 2 < B:
                        if n == AT_XT + BEHIND:
                            copy_xT(b + 2)
                        if n == AT_C + BEHIND:
                            copy_c(b + 2)
                        if n == AT_Q + BEHIND:
                            part1(b + 2, 0)
                        if n == AT_K + BEHIND:
                            part1(b + 2, 1)
                    if u % 2 == 0 and b + 1 < B and n == AT_V + BEHIND:
                        copy_v(b + 1)
                    if u % 2 == 0 and 1 <= b < B:
                        if n == AT_ONT + BEHIND:
                            copy_onT(b - 1)
                        if n == AT_X2T + BEHIND:
                            copy_x2T(b - 1)
                        if n == AT_TOP:
                            top_exp(b - 1)
                    if u % 2 == 1 and 1 <= b < B and n % 4 == (AT_MOE + 3) % 4 and n // 4 < T:
                        weigh_hi(b - 1, n // 4)
                if u + 1 < NU:
                    shift_high(u + 1)
            copy_pv(NU - 1)
            b = B - 1
            copy_onT(b)
            copy_x2T(b)
            top_exp(b)
            for t in range(T):
                weigh_hi(b, t)

        @block.vector
        def _(dve):
            def norm(k, b):
                for t in range(T):
                    dve.bn_stats(ST6[:, k, b, t, :], X[:, b, t, :]).then_inc(s_st[k], 1)
                dve.wait_ge(s_st[k], T * (b + 1))
                for t in range(T):
                    dve.bn_aggr(MV[:, k, b, t, :], ST6[:, k, b, t, :]).then_inc(s_mv[k], 1)
                dve.wait_ge(s_mv[k], T * (b + 1))
                dve.tensor_scalar(VE[:, k, b, :], MV[:, k, b, :, 1], EPS, None, ALU.add).then_inc(s_ve[k], 1)

            def norm_out(k, b):
                dve.wait_ge(s_rs[k], b + 1)
                for t in range(T):
                    dve.tensor_scalar(TOK[:, b, t, :], X[:, b, t, :], MV[:, k, b, t, 0:1],
                                      RS[:, k, b, t:t + 1], ALU.subtract, ALU.mult).then_inc(s_ln[k], 1)

            def zero_rows():
                for o in range(2):
                    dve.memset((QS, KS)[o][0:64, 0, :, :].rearrange("p h n -> p (h n)").bitcast(U32),
                               0).then_inc(s_zero[0], 1)

            def rest(b, o):
                dve.wait_ge(s_p1[o], b + 1)
                if b >= 2:
                    dve.wait_ge(s_qs[b % 2], stacked(b - 2))
                dve.tensor_tensor(RES[:, b % 2, o, :], qk_bank(b, o)[:, :], PT1[:, b % 2, o, :],
                                  ALU.subtract).then_inc(s_r[o], 1)
                dve.wait_ge(s_r[o], b + 1)
                dve.tensor_copy(PT2[:, b % 2, o, :], RES[:, b % 2, o, :]).then_inc(s_p2[o], 1)

            def maxima(u, n):
                F = NMF * u + n
                c, j0, m = FILLS[n]
                dve.wait_ge(s_smf, F + 1)
                if n == 0 and u >= 2:
                    dve.wait_ge(s_smf, NMF * (u - 1))
                dve.tensor_reduce(MX[:, u % 2, j0:j0 + m, c - 1],
                                  SM[F % NSM][:, 0:m * SUB * c].rearrange("p (j w) -> p j w", j=m),
                                  AX.X, ALU.max).then_inc(s_smr, 1)

            def shift_low(u):
                F = NMF * u + NF
                dve.wait_ge(s_hi, u + 1)
                dve.scalar_tensor_tensor(out=SH[:, u % 2, 1, :], in0=SM[F % NSM][0:4 * I, 0:P], scalar=-1.0,
                                         in1=SH[:, u % 2, 0, :], op0=ALU.mult, op1=ALU.subtract
                                         ).then_inc(s_smr, 1)

            def normalise(b, half):
                k = 2 * b + half
                dve.wait_ge(s_otp, k + 1)
                o = MB[:, :].rearrange("p (a c) -> p a c", c=32)
                dve.reciprocal(RL[:, b, half, :, :], o[:, :, 2 * DK:2 * DK + 2]).then_inc(s_rl, 1)
                dve.wait_ge(s_rl, k + 1)
                dve.tensor_tensor(
                    TOK[:, b, 2 * half:2 * half + 2, :].rearrange("p t (a s e) -> p (t a) s e", s=2, e=DK),
                    o[:, :, 0:2 * DK].rearrange("p a (s e) -> p a s e", s=2),
                    RL[:, b, half, :, :].unsqueeze(3).to_broadcast([P, 16, 2, DK]), ALU.mult).then_inc(s_on, 1)

            def residual(b):
                dve.wait_ge(s_yp, b + 1)
                xb = X[:, b, :, :].rearrange("p t d -> p (t d)")
                dve.tensor_tensor(xb, MB[:, :], xb, ALU.add).then_inc(s_x1, 1)
                dve.wait_ge(s_x1, b + 1)

            def router(b):
                if b == 0:
                    dve.wait_ge(s_w, 16 * 10)
                dve.wait_ge(s_lgp, b + 1)
                dve.tensor_tensor(LG[:, b, :, :], MB[:, 0:T * NE].rearrange("p (t e) -> p t e", t=T),
                                  BG[:, :].unsqueeze(1).to_broadcast([P, T, NE]), ALU.add).then_inc(s_lg, 1)
                dve.wait_ge(s_lg, b + 1)
                for t in range(T):
                    dve.max(TOP[:, b, t, :], LG[:, b, t, :]).then_inc(s_top, 1)
                dve.wait_ge(s_top, T * (b + 1))
                dve.tensor_tensor(DF[:, b, :], TOP[:, b, :, 1], TOP[:, b, :, 0], ALU.subtract).then_inc(s_df, 1)
                for t in range(T):
                    dve.max_index(TIX[:, b, t, :], TOP[:, b, t, :], LG[:, b, t, :]).then_inc(s_tix, 1)
                dve.wait_ge(s_tix, T * (b + 1))
                dve.tensor_copy(TIF[:, b, :, :], TIX[:, b, :, 0:2]).then_inc(s_gate, 1)
                dve.wait_ge(s_const, 11)
                dve.wait_ge(s_gate, 8 * b + 1)
                for k in range(2):
                    dve.tensor_tensor(OH[:, b, k, :, :], iota8[:, :].unsqueeze(1).to_broadcast([P, T, NE]),
                                      TIF[:, b, :, k].unsqueeze(2).to_broadcast([P, T, NE]),
                                      ALU.is_equal).then_inc(s_gate, 1)

            def gates(b):
                dve.wait_ge(s_e1, b + 1)
                dve.tensor_scalar(DEN[:, b, :], E1[:, b, :], 1.0, None, ALU.add).then_inc(s_gate, 1)
                dve.wait_ge(s_gate, 8 * b + 4)
                dve.reciprocal(G12[:, b, 0, :], DEN[:, b, :]).then_inc(s_gate, 1)
                dve.wait_ge(s_gate, 8 * b + 5)
                dve.tensor_tensor(G12[:, b, 1, :], E1[:, b, :], G12[:, b, 0, :], ALU.mult).then_inc(s_gate, 1)
                dve.wait_ge(s_gate, 8 * b + 6)
                for k in range(2):
                    dve.tensor_tensor(GW[:, b, k, :, :], OH[:, b, k, :, :],
                                      G12[:, b, k, :].unsqueeze(2).to_broadcast([P, T, NE]),
                                      ALU.mult).then_inc(s_gate, 1)
                dve.wait_ge(s_gate, 8 * b + 8)
                dve.tensor_tensor(G[:, b, :, :], GW[:, b, 0, :, :], GW[:, b, 1, :, :], ALU.add).then_inc(s_g, 1)

            def bias_parts():
                dve.wait_ge(s_b, 1)
                dve.tensor_tensor(BR[:, :], BE[:, :], BP[:, 0, :], ALU.subtract).then_inc(s_b, 1)
                dve.wait_ge(s_b, 2)
                dve.tensor_copy(BP[:, 1, :], BR[:, :]).then_inc(s_b, 1)
                dve.wait_ge(s_b, 3)
                dve.tensor_tensor(BE[:, :], BR[:, :], BP[:, 1, :], ALU.subtract).then_inc(s_b, 1)
                dve.wait_ge(s_b, 4)
                dve.tensor_copy(BP[:, 2, :], BE[:, :]).then_inc(s_b, 1)

            def weigh_lo(b, t):
                n = T * b + t
                dve.wait_ge(s_mep[0], n + 1)
                dve.wait_ge(s_g, b + 1)
                if n >= 2:
                    dve.wait_ge(s_o, n - 1)
                dve.tensor_tensor(PROD[:, n % 2, 0:4, :], expert_bank(b, t, 0)[:, :].rearrange("p (e o) -> p e o", e=4),
                                  G[:, b, t, 0:4].unsqueeze(2).to_broadcast([P, 4, DO]),
                                  ALU.mult).then_inc(s_me[0], 1)

            dve.wait_ge(s_x[0], 16)
            norm(0, 0)
            norm_out(0, 0)
            zero_rows()
            rest(0, 0)
            rest(0, 1)
            bias_parts()
            for u in range(-1, NU):
                b = u // 2
                for n in range(NF):
                    if u + 1 < NU:
                        maxima(u + 1, n)
                    if u % 2 == 1 and 1 <= b < B and n % 4 == (AT_MOE + 1) % 4 and n // 4 < T:
                        weigh_lo(b - 1, n // 4)
                    if u % 2 == 1 and b + 2 < B:
                        if n == AT_LN1:
                            dve.wait_ge(s_x[b + 2], 16)
                            norm(0, b + 2)
                        if n == AT_LN1OUT:
                            norm_out(0, b + 2)
                        if n == AT_Q + BEHIND:
                            rest(b + 2, 0)
                        if n == AT_K + BEHIND:
                            rest(b + 2, 1)
                    if u % 2 == 0 and 1 <= b < B:
                        if n == AT_OT0 + BEHIND:
                            normalise(b - 1, 0)
                        if n == AT_OT1 + BEHIND:
                            normalise(b - 1, 1)
                        if n == AT_Y + BEHIND:
                            residual(b - 1)
                            norm(1, b - 1)
                        if n == AT_LN2OUT:
                            norm_out(1, b - 1)
                        if n == AT_LOG + BEHIND:
                            router(b - 1)
                        if n == AT_GATE:
                            gates(b - 1)
                if u + 1 < NU:
                    shift_low(u + 1)
            b = B - 1
            normalise(b, 0)
            normalise(b, 1)
            residual(b)
            norm(1, b)
            norm_out(1, b)
            router(b)
            gates(b)
            for t in range(T):
                weigh_lo(b, t)


_INS = ["L0_attn_x", "L0_attn_W_dq", "L0_attn_W_uq", "L0_attn_W_dkv", "L0_attn_W_uk", "L0_attn_W_uv",
        "L0_attn_W_o", "L0_ffn_We", "L0_ffn_be", "L0_ffn_Wg", "L0_ffn_bg"]


def kernel(**inputs):
    import numpy as _np
    import concourse.bacc as _bacc
    from concourse import mybir as _mybir
    from concourse.bass_utils import run_bass_kernel_spmd as _run

    nc = _bacc.Bacc("TRN2", target_bir_lowering=False, num_devices=1)
    arrays, args = {}, []
    for name in _INS:
        a = _np.ascontiguousarray(inputs[name])
        arrays[f"in_{name}_dram"] = a
        args.append(nc.dram_tensor(f"in_{name}_dram", a.shape, _mybir.dt.from_np(a.dtype), kind="ExternalInput").ap())
    shape = inputs["L0_attn_x"].shape
    args.append(nc.dram_tensor("out_0_dram", shape, _mybir.dt.float32, kind="ExternalOutput").ap())
    build(nc, *args)
    r = _run(nc, [arrays], core_ids=[0])
    return r.results[0]["out_0_dram"]
```

```python
from contextlib import ExitStack

import concourse.bass as bass
from concourse import mybir

F32 = mybir.dt.float32
BF16 = mybir.dt.bfloat16
U32 = mybir.dt.uint32
ALU = mybir.AluOpType
ACT = mybir.ActivationFunctionType
AX = mybir.AxisListType

P = 128
SUB = 64
EPS = 1e-5
BIG = 1e30
PARTS = ((0, 0), (0, 1), (1, 0), (0, 2), (2, 0), (1, 1))

LAG = 5
PV_BEHIND = 3
NSM = 3
WARM = (4, 3, 2, 1)

PREP = dict(ln1=3, ln1_var=9, ln1_out=11, ln1_out2=12, xT=15, q=19, k=21, stack=29, v=33)
PREP_ROW1 = dict(ln1=9, ln1_var=10, ln1_out=15, ln1_out2=17, xT=21, q=26, k=28, stack=31, v=37)
POST = dict(oT0=6, oT1=8, onT=9, y=11, ln2=11, ln2_var=12, ln2_out=15, ln2_out2=15, x2T=18, logits=21, index=21, top=21, gates=21, gates2=23)
MOE = (0, 2)
LATE = dict(xT=1, q=0, k=2, q_rest=0, k_rest=2, oT0=0, oT1=0, onT=0, y=0, x2T=0, logits=0, v=2, lo=2, hi=0, hi2=2)


def fill_plan(SUBS, bank):
    plan = []
    for c in range(SUBS, 0, -1):
        m = min(4, bank // (SUB * c))
        m = 4 if m == 3 else m
        m = 2 if m == 2 else m
        for j in range(0, 4, m):
            plan.append((c, j, m))
    return plan


def build(nc, x, W_dq, W_uq, W_dkv, W_uk, W_uv, W_o, We, be, Wg, bg, out):
    B, S, D = x.shape
    C = W_dq.shape[1]
    NE, _, DO = We.shape
    H = 16
    DK = D // H
    T = S // P
    I = S // SUB
    NP = H // 2
    NU = 2 * B
    SCALE = float(DK) ** -0.5
    FILLS = fill_plan(I, S)
    NF = len(FILLS)
    NMF = NF + 1
    ZEROED = 6
    NDMA = len(PARTS) * 2 + 1

    with ExitStack() as ctx:
        def sb(name, shape, dt):
            return ctx.enter_context(nc.sbuf_tensor(name, shape, dt))

        def pb(name):
            return ctx.enter_context(nc.psum_tensor(name, [P, 512], F32))

        def sem(name):
            return ctx.enter_context(nc.semaphore(name))

        QS = sb("QS", [P, 2, H, S], BF16)
        KS = sb("KS", [P, 2, H, S], BF16)
        VB = sb("VB", [P, 2, I, NP, 32], F32)
        PR = sb("PR", [P, 2, 4, S], F32)
        X = sb("X", [P, B, T, D], F32)
        TOK = sb("TOK", [P, B, T, D], F32)
        FT = sb("FT", [P, B, T, P], F32)
        OT = sb("OT", [P, 2, 2, S], F32)
        PT1 = sb("PT1", [P, 2, 2, S], BF16)
        PT2 = sb("PT2", [P, 2, 2, S], BF16)
        PT3 = sb("PT3", [P, 2, 2, S], BF16)
        RES = sb("RES", [P, 2, 2, S], F32)
        MX = sb("MX", [P, 2, 4, I], F32)
        SH = sb("SH", [8 * I, 2, P], BF16)
        Wd = sb("Wd", [P, 2 * C], F32)
        Wu = sb("Wu", [2 * C, 2, P], F32)
        WP = sb("WP", [2 * C, P], F32)
        WdT = sb("WdT", [2 * C, P], F32)
        WF = sb("WF", [P, 3, P], F32)
        Wo = sb("Wo", [P, D], F32)
        WE = sb("WE", [P, NE, DO], F32)
        BE = sb("BE", [1, NE * DO], F32)
        BR = sb("BR", [1, NE * DO], F32)
        BP = sb("BP", [1, 3, NE * DO], BF16)
        BEP = sb("BEP", [P, NE * DO], BF16)
        WG = sb("WG", [P, NE], F32)
        BG = sb("BG", [P, NE], F32)
        ident = sb("ident", [P, P], F32)
        identb = sb("identb", [P, P], BF16)
        MSK = sb("MSK", [P, 2, SUB], BF16)
        ZR = sb("ZR", [P, S], BF16)
        ON = sb("ON", [P, S], BF16)
        mhalf = sb("mhalf", [P, T], F32)
        iota8 = sb("iota8", [P, NE], F32)
        ST6 = sb("ST6", [P, 2, B, T, 6], F32)
        MV = sb("MV", [P, 2, B, T, 2], F32)
        VE = sb("VE", [P, 2, B, T], F32)
        RS = sb("RS", [P, 2, B, T], F32)
        RL = sb("RL", [P, B, 2, 16, 2], F32)
        LG = sb("LG", [P, B, T, NE], F32)
        TOP = sb("TOP", [P, B, T, 8], F32)
        TIX = sb("TIX", [P, B, T, 8], U32)
        TIF = sb("TIF", [P, B, T, 2], F32)
        DF = sb("DF", [P, B, T], F32)
        E1 = sb("E1", [P, B, T], F32)
        DEN = sb("DEN", [P, B, T], F32)
        G12 = sb("G12", [P, B, 2, T], F32)
        OH = sb("OH", [P, B, 2, T, NE], F32)
        GW = sb("GW", [P, B, 2, T, NE], F32)
        G = sb("G", [P, B, T, NE], F32)
        PROD = sb("PROD", [P, 2, NE, DO], F32)

        SM = [pb(f"SM{n}") for n in range(NSM)]
        SA = [pb("SA0"), pb("SA1")]
        PV = pb("PV")
        MA = pb("MA")
        MB = pb("MB")

        s_wq = sem("projection_weights_in")
        s_w = sem("weights_in")
        s_be = sem("expert_biases_in")
        s_wdp = sem("down_weights_turned")
        s_wd = sem("down_weights_copied")
        s_wfp = sem("weight_products_in_psum")
        s_wf = sem("weight_products_copied")
        s_wp = sem("up_weights_permuted")
        s_x = [sem(f"x_in{b}") for b in range(B)]
        s_const = sem("constants_made")
        s_on1 = sem("one_rows_made")
        s_vz = sem("value_zeros_made")
        s_vone = sem("value_ones_made")
        s_pad = [sem("pad_rows_in0"), sem("pad_rows_in1")]
        s_zero = [sem("zero_rows_made0"), sem("zero_rows_made1")]
        s_st = [sem("ln1_stats"), sem("ln2_stats")]
        s_mv = [sem("ln1_meanvar"), sem("ln2_meanvar")]
        s_ve = [sem("ln1_var_eps"), sem("ln2_var_eps")]
        s_rs = [sem("ln1_rstd"), sem("ln2_rstd")]
        s_ln = [sem("ln1_out"), sem("ln2_out")]
        s_xtp = sem("xT_in_psum")
        s_xt = sem("xT_copied")
        s_pp = [sem("q_in_psum"), sem("k_in_psum")]
        s_p1 = [sem("q_part1"), sem("k_part1")]
        s_r = [sem("q_rest"), sem("k_rest")]
        s_p2 = [sem("q_part2"), sem("k_part2")]
        s_p3 = [sem("q_part3"), sem("k_part3")]
        s_vp = sem("v_in_psum")
        s_v = sem("v_copied")
        s_qs = [sem("stacked_in0"), sem("stacked_in1")]
        s_first = sem("first_k_parts_of_row0_in")
        s_smf = sem("max_bank_filled")
        s_smr = sem("max_bank_read")
        s_hi = sem("shift_high")
        s_sh = [sem("shift_rows_in0"), sem("shift_rows_in1")]
        s_saf = sem("att_bank_filled")
        s_exp = sem("exp_done")
        s_pv = sem("pv_done")
        s_ot = sem("pv_copied")
        s_otp = sem("oT_in_psum")
        s_rl = sem("recip_done")
        s_on = sem("o_normalised")
        s_ontp = sem("onT_in_psum")
        s_ont = sem("onT_copied")
        s_yp = sem("y_in_psum")
        s_x1 = sem("x1_done")
        s_x2tp = sem("x2T_in_psum")
        s_x2t = sem("x2T_copied")
        s_lgp = sem("logits_in_psum")
        s_lg = sem("logits_done")
        s_top = sem("top8_done")
        s_tix = sem("top8_index_done")
        s_df = sem("top_difference")
        s_e1 = sem("top_exp")
        s_gate = sem("gate_steps")
        s_g = sem("gates_done")
        s_b = sem("bias_steps")
        s_bz = sem("bias_zero_rows_made")
        s_bin = sem("bias_rows_in")
        s_mep = [sem("experts_lo_in_psum"), sem("experts_hi_in_psum")]
        s_me = [sem("experts_lo_weighted"), sem("experts_hi_weighted")]
        s_sum = [sem("expert_sums_even"), sem("expert_sums_odd")]
        s_o = [sem("even_tile_out"), sem("odd_tile_out")]
        s_store = sem("stored")

        block = ctx.enter_context(nc.Block())

        def qk_bank(b, o):
            return MB if (b, o) == (0, 1) else MA

        WHOLE = ((0, T),)
        HALVES = ((0, T // 2), (T // 2, T // 2))

        def tiles(b, part):
            return T * b + part[0] + part[1]

        def turn(b, part):
            return b + part[0] // 2

        def due(step, now, late=0):
            rows = []
            for r in range(B):
                if step in PREP and r == 1 and now - late == PREP_ROW1[step]:
                    rows.append(r)
                if step in PREP and r >= 2 and now - late == PREP[step] + NF * (2 * r - 2):
                    rows.append(r)
                if step in POST and r < B - 1 and now - late == POST[step] + NF * (2 * r + 3):
                    rows.append(r)
            return rows

        def experts_due(now, late=0):
            return [(r, k) for r in range(B - 1) for k in range(2 * T)
                    if now - late == MOE[0] + MOE[1] * k + NF * (2 * r + 4)]

        def ends_class(a):
            return a % NF == NF - 1 or FILLS[a % NF][0] != FILLS[a % NF + 1][0]

        def att_bank(u, n):
            return SA[(NF * u + n) % 2] if u < NU - 1 else [SA[0], SA[1], SM[2], SM[1]][n % 4]

        def post_bank(b, part):
            return MB if b < B - 1 else SM[part[0] // 2]

        def products(b, t):
            if b == B - 1 and t >= 2:
                return RES[:, t - 2, :, :].rearrange("p o s -> p (o s)").rearrange("p (e n) -> p e n", e=NE)
            return PROD[:, (T * b + t) % 2, :, :]

        def expert_bank(b, k):
            if b < B - 1:
                return (MA, MB)[k % 2]
            return [MA, MB, SM[2], SA[0], SA[1], PV, SM[0], SM[1]][k]

        def stacked(b):
            return 16 * (NDMA * (b // 2 + 1) - (3 if b % 2 == 0 else 0))

        def spread(engine, b, level, o, done):
            engine.wait_ge((s_p1, s_p2, s_p3)[level][o], b + 1)
            src = (PT1, PT2, PT3)[level][:, b % 2, o, :]
            for n, pair in enumerate(PARTS):
                if pair[o] == level:
                    r = 64 + 8 * n
                    engine.dma_start((QS, KS)[o][r:r + 8, b % 2, :, :], src).then_inc(done, 16)

        @block.sync
        def _(sp):
            def load_x(b):
                sp.dma_start(X[:, b, :, :], x[b].rearrange("(t p) d -> p t d", p=P)).then_inc(s_x[b], 16)

            def pad_rows(par):
                sp.dma_start(QS[120:128, par, :, :], ZR[:, :]).then_inc(s_pad[par], 16)
                sp.dma_start(KS[112:120, par, :, :], ON[:, :]).then_inc(s_pad[par], 16)
                sp.dma_start(KS[120:128, par, :, :], ZR[:, :]).then_inc(s_pad[par], 16)

            def zero_rows(par):
                for o in range(2):
                    sp.dma_start((QS, KS)[o][0:64, par, :, :],
                                 ZR[0:64, :].unsqueeze(1).to_broadcast([64, H, S])).then_inc(s_zero[par], 16)

            def stack(b):
                if b >= 2:
                    sp.wait_ge(s_saf, NF * 2 * (b - 1))
                sp.dma_start(QS[112:120, b % 2, :, :], ZR[:, :]).then_inc(s_qs[b % 2], 16)
                for level in range(3):
                    for o in range(2):
                        if b > 0 or (level, o) != (0, 1):
                            spread(sp, b, level, o, s_qs[b % 2])

            def shift_rows(u):
                sp.wait_ge(s_smr, NMF * (u + 1))
                g = u % 2
                for s in range(2):
                    h = NP * s + 4 * g
                    sp.dma_start(QS[112:114, (u // 2) % 2, h:h + 4, :],
                                 SH[:, u % 2, SUB * s:SUB * s + SUB]).then_inc(s_sh[u % 2], 16)

            def store(b, t):
                sp.wait_ge(s_o[t % 2], (T * b + t) // 2 + 1)
                sp.dma_start(out[b, t * P:(t + 1) * P, :], TOK[:, b, t, :]).then_inc(s_store, 16)

            load_x(0)
            sp.dma_start(Wu[0:C, 0, :], W_uq).then_inc(s_wq, 16)
            sp.dma_start(Wu[C:2 * C, 0, :], W_uk).then_inc(s_wq, 16)
            sp.dma_start(Wu[C:2 * C, 1, :], W_uv).then_inc(s_wq, 16)
            sp.wait_ge(s_const, 1)
            sp.dma_start(KS[0:64, 0, ZEROED:H, :], ZR[0:64, :].unsqueeze(1).to_broadcast([64, H - ZEROED, S])
                         ).then_inc(s_pad[0], 16)
            sp.wait_ge(s_on1, 1)
            pad_rows(0)
            sp.dma_start(BE[:, :], be.rearrange("(a e) o -> a (e o)", a=1)).then_inc(s_be, 16)
            stack(0)
            load_x(1)
            pad_rows(1)
            zero_rows(1)
            load_x(2)
            load_x(3)
            sp.dma_start(Wo[:, :], W_o).then_inc(s_w, 16)
            sp.dma_start(WG[:, :], Wg).then_inc(s_w, 16)
            sp.dma_start(BG[:, :], bg.partition_broadcast(P)).then_inc(s_w, 16)
            sp.dma_start(WE[:, :, :], We.rearrange("e d o -> d e o")).then_inc(s_w, 16)
            sp.wait_ge(s_bz, 1)
            sp.wait_ge(s_b, 5)
            for n in range(3):
                sp.dma_start(BEP[n:n + 1, :], BP[0:1, n, :]).then_inc(s_bin, 16)
            for now in range(NF * (NU + 1)):
                for b in due("stack", now):
                    stack(b)
                for b, k in experts_due(now, 3):
                    if k % 2:
                        store(b, k // 2)
                if now % NF == NF - 1 and now // NF < NU:
                    shift_rows(now // NF)
            for t in range(T):
                store(B - 1, t)
            sp.wait_ge(s_store, 16 * B * T)

        @block.gpsimd
        def _(pool):
            pool.memset(ZR[:, :], 0.0).then_inc(s_const, 1)
            pool.memset(ON[:, :], 0.0).then_inc(s_const, 1)
            pool.memset(ident[:, :], 0.0).then_inc(s_const, 1)
            pool.memset(mhalf[:, :], -0.5).then_inc(s_const, 1)
            pool.wait_ge(s_const, 4)
            pool.memset(ON[0:32, :], 1.0).then_inc(s_on1, 1)
            pool.wait_ge(s_on1, 1)
            pool.affine_select(out=ident[:, :], in_=ident[:, :], compare_op=ALU.not_equal, fill=1.0, base=0,
                               pattern=[[-1, P]], channel_multiplier=1).then_inc(s_const, 1)
            pool.affine_select(out=identb[:, :], in_=ZR[:, 0:P], compare_op=ALU.not_equal, fill=1.0, base=0,
                               pattern=[[-1, P]], channel_multiplier=1).then_inc(s_const, 1)
            for o, sign in ((0, 1), (1, -1)):
                pool.affine_select(out=MSK[:, o, :], in_=ZR[:, 0:SUB], compare_op=ALU.is_ge, fill=-BIG,
                                   base=-SUB * sign, pattern=[[-sign, SUB]],
                                   channel_multiplier=sign).then_inc(s_const, 1)
            pool.wait_ge(s_const, 8)
            for o, sign in ((0, 1), (1, -1)):
                pool.affine_select(out=MSK[0:SUB, o, :], in_=ZR[0:SUB, 0:SUB], compare_op=ALU.is_ge, fill=-BIG,
                                   base=0, pattern=[[-sign, SUB]], channel_multiplier=sign).then_inc(s_const, 1)
            pool.wait_ge(s_const, 10)
            pool.iota(iota8[:, :], pattern=[[1, NE]], base=0, channel_multiplier=0,
                      allow_small_or_imprecise_dtypes=True).then_inc(s_const, 1)

            def rstd(k, b, part=WHOLE[0]):
                pool.wait_ge(s_ve[k], tiles(b, part))
                t = slice(part[0], part[0] + part[1])
                pool.tensor_tensor(RS[:, k, b, t], VE[:, k, b, t], mhalf[:, t], ALU.pow).then_inc(s_rs[k], part[1])

            def third_part(b, o):
                pool.wait_ge(s_p2[o], b + 1)
                if b >= 2:
                    pool.wait_ge(s_qs[b % 2], stacked(b - 2))
                pool.tensor_tensor(PT3[:, b % 2, o, :], RES[:, b % 2, o, :], PT2[:, b % 2, o, :],
                                   ALU.subtract).then_inc(s_p3[o], 1)

            def expert_sums(b, t):
                n = T * b + t
                pr, o, v = products(b, t), n % 2, n // 2
                pool.wait_ge(s_me[0], n + 1)
                pool.wait_ge(s_me[1], n + 1)
                pool.tensor_tensor(pr[:, 0:4, :], pr[:, 0:4, :], pr[:, 4:8, :], ALU.add).then_inc(s_sum[o], 1)
                pool.wait_ge(s_sum[o], 3 * v + 1)
                pool.tensor_tensor(pr[:, 0:2, :], pr[:, 0:2, :], pr[:, 2:4, :], ALU.add).then_inc(s_sum[o], 1)
                pool.wait_ge(s_sum[o], 3 * v + 2)
                pool.tensor_tensor(pr[:, 0, :], pr[:, 0, :], pr[:, 1, :], ALU.add).then_inc(s_sum[o], 1)
                pool.wait_ge(s_sum[o], 3 * v + 3)
                pool.wait_ge(s_x1, tiles(b, WHOLE[0]) if b < B - 1 else tiles(b, HALVES[t // 2]))
                pool.tensor_tensor(TOK[:, b, t, :], pr[:, 0, :], X[:, b, t, :], ALU.add).then_inc(s_o[o], 1)

            rstd(0, 0)
            pool.memset(VB[:, :, :, :, :], 0.0).then_inc(s_vz, 1)
            pool.wait_ge(s_vz, 1)
            pool.memset(VB[0:SUB, :, :, :, 2 * DK:2 * DK + 1], 1.0).then_inc(s_vone, 1)
            pool.wait_ge(s_vone, 1)
            pool.memset(VB[SUB:P, :, :, :, 2 * DK + 1:2 * DK + 2], 1.0).then_inc(s_vone, 1)
            pool.wait_ge(s_vone, 2)
            spread(pool, 0, 0, 1, s_first)
            pool.memset(BEP[:, :], 0.0).then_inc(s_bz, 1)
            for now in range(NF * (NU + 1)):
                for b in due("ln1_var", now):
                    rstd(0, b)
                for b in due("ln2_var", now):
                    rstd(1, b)
                for b in due("q", now):
                    third_part(b, 0)
                for b in due("k", now):
                    third_part(b, 1)
                for b, k in experts_due(now, 1):
                    if k % 2:
                        expert_sums(b, k // 2)
            rstd(1, B - 1, HALVES[0])
            rstd(1, B - 1, HALVES[1])
            for t in range(0, T, 2):
                expert_sums(B - 1, t)

        @block.tensor
        def _(pe):
            def xT(b):
                pe.wait_ge(s_const, 5)
                pe.wait_ge(s_ln[0], T * (b + 1))
                if b >= 1:
                    pe.wait_ge(s_v, 2 * b)
                if b >= 3:
                    pe.wait_ge(s_me[0], T * (b - 2))
                for t in range(T):
                    last = pe.transpose(MA[:, t * P:(t + 1) * P], TOK[:, b, t, :], ident[:, :])
                last.then_inc(s_xtp, 1)

            def keep_warm(n):
                for _ in range(WARM[n]):
                    pe.matmul(SM[0][:, :], identb[:, :], ZR[:, :], start=True, stop=True)

            def turn_down_weights():
                pe.wait_ge(s_wq, 16 * 5)
                pe.transpose(MB[0:2 * C, 0:P], Wd[:, :], ident[:, :]).then_inc(s_wdp, 1)

            def multiply_weights():
                pe.wait_ge(s_wd, 1)
                pe.wait_ge(s_wp, 1)
                for n, (side, up_weights) in enumerate(((0, WP[0:C, :]), (1, WP[C:2 * C, :]), (1, Wu[C:2 * C, 1, :]))):
                    pe.matmul((SM[1], MB, MB)[n][:, P * n:P * (n + 1)], WdT[C * side:C * side + C, :], up_weights,
                              start=True, stop=True).then_inc(s_wfp, 1)

            def up(b, o):
                pe.wait_ge(s_xt, b + 1)
                if o == 1 and b >= 1:
                    pe.wait_ge(s_r[0], b + 1)
                if b == 0:
                    pe.wait_ge(s_wf, 2)
                pe.matmul(qk_bank(b, o)[:, :], WF[:, o, :], FT[:, b, :, :].rearrange("p t n -> p (t n)"),
                          start=True, stop=True).then_inc(s_pp[o], 1)

            def values(b):
                pe.wait_ge(s_r[0 if b == 0 else 1], b + 1)
                w = WF[:, 2, :].rearrange("k (p s e) -> k s p e", s=2, e=DK)
                xT = FT[:, b, :, :].rearrange("p t n -> p (t n)")
                for i in range(I):
                    for s in range(2):
                        last = pe.matmul(MA[SUB * s:SUB * s + SUB, SUB * i:SUB * i + SUB],
                                         xT[:, SUB * i:SUB * i + SUB], w[:, s], start=True, stop=True)
                last.then_inc(s_vp, 1)

            def max_fill(u, n):
                b, g, F = u // 2, u % 2, NMF * u + n
                if n == 0 and g == 0:
                    pe.wait_ge(s_qs[b % 2], stacked(b))
                    pe.wait_ge(s_first, 48)
                    pe.wait_ge(s_zero[b % 2], 32 if b % 2 else (H + ZEROED) // 2)
                    pe.wait_ge(s_const, 10)
                    pe.wait_ge(s_pad[b % 2], 48 if b % 2 else 64)
                if F >= NSM:
                    pe.wait_ge(s_smr, F - NSM + 1)
                c, j0, m = FILLS[n]
                i, bank = c - 1, SM[F % NSM]
                for j in range(m):
                    for s in range(2):
                        h = NP * s + 4 * g + j0 + j
                        pe.matmul(bank[SUB * s:SUB * s + SUB, SUB * c * j:SUB * c * (j + 1)],
                                  QS[:, b % 2, h, SUB * i:SUB * c], KS[:, b % 2, h, 0:SUB * c],
                                  start=(j == 0), stop=False, skip_group_check=True)
                last = pe.matmul(bank[:, 0:m * SUB * c].rearrange("p (j w) -> p j w", j=m)[:, :, SUB * i:SUB * c],
                                 identb[:, :], MSK[:, 0, :].unsqueeze(1).to_broadcast([P, m, SUB]),
                                 start=False, stop=True, skip_group_check=True)
                last.then_inc(s_smf, 1)

            def max_turn(u):
                F = NMF * u + NF
                pe.wait_ge(s_smr, F)
                for copy in range(2):
                    last = pe.matmul(SM[F % NSM][4 * I * copy:4 * I * (copy + 1), 0:P],
                                     MX[:, u % 2, :, :].rearrange("p j i -> p (j i)"), ident[:, :], start=True, stop=True)
                last.then_inc(s_smf, 1)

            def att_fill(u, n):
                b, g, F = u // 2, u % 2, NF * u + n
                if n == 0:
                    pe.wait_ge(s_sh[u % 2], 32 * (u // 2 + 1))
                if F >= 2 and (u < NU - 1 or n < 2):
                    pe.wait_ge(s_exp, F - 1)
                if u == NU - 1 and n == 2:
                    pe.wait_ge(s_smr, NMF * NU)
                if u == NU - 1 and n >= 4:
                    pe.wait_ge(s_exp, F - 3)
                c, j0, m = FILLS[n]
                i, bank = I - c, att_bank(u, n)
                for j in range(m):
                    for s in range(2):
                        h = NP * s + 4 * g + j0 + j
                        pe.matmul(bank[SUB * s:SUB * s + SUB, SUB * c * j:SUB * c * (j + 1)],
                                  KS[:, b % 2, h, SUB * i:SUB * i + SUB], QS[:, b % 2, h, SUB * i:S],
                                  start=(j == 0), stop=False, skip_group_check=True)
                last = pe.matmul(bank[:, 0:m * SUB * c].rearrange("p (j w) -> p j w", j=m)[:, :, 0:SUB],
                                 identb[:, :], MSK[:, 1, :].unsqueeze(1).to_broadcast([P, m, SUB]),
                                 start=False, stop=True, skip_group_check=True)
                last.then_inc(s_saf, 1)

            def pv(u, i):
                b, g = u // 2, u % 2
                done = sum(1 for c, _, _ in FILLS if I - c <= i)
                pe.wait_ge(s_exp, NF * u + done)
                if i == 0:
                    pe.wait_ge(s_v, 2 * (b + 1))
                    pe.wait_ge(s_vone, 2)
                if i == 0 and u >= 1:
                    pe.wait_ge(s_ot, u)
                if u == NU - 1 and i == I // 2:
                    pe.wait_ge(s_ot, NU)
                for j in range(4):
                    last = pe.matmul(PV[32 * j:32 * j + 32, SUB * i:S], VB[:, b % 2, i, 4 * g + j, :],
                                     PR[:, i % 2, j, 0:S - SUB * i], start=(i == 0),
                                     stop=(i == I - 1 or (u == NU - 1 and i == I // 2 - 1)), skip_group_check=(u == NU - 1))
                last.then_inc(s_pv, 1)

            def oT(b, half):
                pe.wait_ge(s_ot, 2 * b + 2 + (b == B - 1 and half == 1))
                if b == B - 1 and half == 0:
                    pe.wait_ge(s_smr, NMF * NU)
                if b < B - 1 and half:
                    pe.wait_ge(s_on, T * b + 2)
                if 1 <= b < B - 1 and not half:
                    pe.wait_ge(s_me[1], T * b)
                bank = post_bank(b, HALVES[half])
                for tt in range(2):
                    t = 2 * half + tt
                    for g in range(2):
                        last = pe.transpose(bank[:, (2 * tt + g) * P:(2 * tt + g + 1) * P],
                                            OT[:, b % 2, g, t * P:(t + 1) * P], ident[:, :])
                last.then_inc(s_otp, 2)

            def onT(b, part=WHOLE[0]):
                pe.wait_ge(s_on, tiles(b, part))
                for t in range(part[0], part[0] + part[1]):
                    last = pe.transpose(post_bank(b, part)[:, t * P:(t + 1) * P], TOK[:, b, t, :], ident[:, :])
                last.then_inc(s_ontp, part[1])

            def y(b, part=WHOLE[0]):
                if b == 0:
                    pe.wait_ge(s_w, 16 * 4)
                pe.wait_ge(s_ont, tiles(b, part))
                for t in range(part[0], part[0] + part[1]):
                    last = pe.matmul(post_bank(b, part)[:, t * D:(t + 1) * D], FT[:, b, t, :], Wo[:, :],
                                     start=True, stop=True)
                last.then_inc(s_yp, part[1])

            def x2T(b, part=WHOLE[0]):
                pe.wait_ge(s_ln[1], tiles(b, part))
                for t in range(part[0], part[0] + part[1]):
                    last = pe.transpose(post_bank(b, part)[:, t * P:(t + 1) * P], TOK[:, b, t, :], ident[:, :])
                last.then_inc(s_x2tp, part[1])

            def logits(b, part=WHOLE[0]):
                pe.wait_ge(s_x2t, tiles(b, part))
                for t in range(part[0], part[0] + part[1]):
                    last = pe.matmul(post_bank(b, part)[:, t * NE:(t + 1) * NE], FT[:, b, t, :], WG[:, :],
                                     start=True, stop=True)
                last.then_inc(s_lgp, part[1])

            def expert_biases(b, k):
                t, half = k // 2, k % 2
                n = T * b + t
                if b == 0 and k == 0:
                    pe.wait_ge(s_bin, 48)
                if b < B - 1 and t == 0:
                    if half == 0 and b + 2 < B:
                        pe.wait_ge(s_v, 2 * (b + 3))
                    if half == 1:
                        pe.wait_ge(s_lg, T * (b + 1))
                if n >= 1 and (b < B - 1 or t == 0):
                    pe.wait_ge(s_me[half], n)
                if b == B - 1 and k == 2:
                    pe.wait_ge(s_exp, NF * NU)
                    pe.wait_ge(s_ot, NU + 1)
                if b == B - 1 and k >= 6:
                    pe.wait_ge(s_lg, tiles(b, HALVES[k - 6]))
                cols = slice(4 * DO * half, 4 * DO * (half + 1))
                pe.matmul(expert_bank(b, k)[:, :], ON[:, 0:P], BEP[:, cols], start=True, stop=False)

            def experts(b, k):
                t, half = k // 2, k % 2
                cols = slice(4 * DO * half, 4 * DO * (half + 1))
                pe.matmul(expert_bank(b, k)[:, :], FT[:, b, t, :], WE[:, :, :].rearrange("p e n -> p (e n)")[:, cols],
                          start=False, stop=True).then_inc(s_mep[half], 1)

            pe.wait_ge(s_const, 7)
            keep_warm(0)
            turn_down_weights()
            keep_warm(1)
            multiply_weights()
            keep_warm(2)
            xT(0)
            keep_warm(3)
            up(0, 0)
            up(0, 1)
            values(0)
            for u in range(-1, NU + 1):
                for n in range(NF if u < NU else LAG):
                    now = NF * (u + 1) + n
                    a = NF * u + n - LAG
                    if a >= 0:
                        att_fill(a // NF, a % NF)
                    if u + 1 < NU:
                        max_fill(u + 1, n)
                    for full in (a - 1, a - PV_BEHIND):
                        last_unit = full >= NF * (NU - 1)
                        if full >= 0 and ends_class(full) and last_unit == (full == a - PV_BEHIND):
                            pv(full // NF, I - FILLS[full % NF][0])
                    for r, k in experts_due(now):
                        expert_biases(r, k)
                        experts(r, k)
                    for r in due("oT0", now):
                        oT(r, 0)
                    for r in due("oT1", now):
                        oT(r, 1)
                    for r in due("onT", now):
                        onT(r)
                    for r in due("y", now):
                        y(r)
                    for r in due("x2T", now):
                        x2T(r)
                    for r in due("logits", now):
                        logits(r)
                    for r in due("xT", now):
                        xT(r)
                    for r in due("q", now):
                        up(r, 0)
                    for r in due("k", now):
                        up(r, 1)
                    for r in due("v", now):
                        values(r)
                    if u == NU and n == 2:
                        oT(B - 1, 0)
                    if u == NU and n == 4:
                        onT(B - 1, HALVES[0])
                if u + 1 < NU:
                    max_turn(u + 1)
            for full in range(NF * NU - PV_BEHIND, NF * NU):
                if full == NF * NU - 1:
                    y(B - 1, HALVES[0])
                if ends_class(full):
                    pv(NU - 1, I - FILLS[full % NF][0])
            b = B - 1
            oT(b, 1)
            for k in range(2):
                expert_biases(b, k)
            x2T(b, HALVES[0])
            onT(b, HALVES[1])
            for k in range(2, 6):
                expert_biases(b, k)
            logits(b, HALVES[0])
            y(b, HALVES[1])
            for k in range(4):
                experts(b, k)
            x2T(b, HALVES[1])
            logits(b, HALVES[1])
            for k in range(4, 2 * T):
                if k >= 6:
                    expert_biases(b, k)
                experts(b, k)

        @block.scalar
        def _(act):
            act.dma_start(Wd[:, 0:C], W_dq).then_inc(s_wq, 16)
            act.dma_start(Wd[:, C:2 * C], W_dkv).then_inc(s_wq, 16)

            def copy_xT(b):
                act.wait_ge(s_xtp, b + 1)
                act.copy(FT[:, b, :, :].rearrange("p t n -> p (t n)"), MA[:, :]).then_inc(s_xt, 1)

            def part1(b, o):
                act.wait_ge(s_pp[o], b + 1)
                if b >= 2:
                    act.wait_ge(s_qs[b % 2], stacked(b - 2))
                act.copy(PT1[:, b % 2, o, :], qk_bank(b, o)[:, :]).then_inc(s_p1[o], 1)

            def copy_v(b):
                act.wait_ge(s_vp, b + 1)
                act.wait_ge(s_vone, 2)
                if b >= 2:
                    act.wait_ge(s_pv, I * 2 * (b - 1))
                for s in range(2):
                    act.copy(VB[SUB * s:SUB * s + SUB, b % 2, :, :, DK * s:DK * s + DK],
                             MA[SUB * s:SUB * s + SUB, :].rearrange("k (i p e) -> k i p e", i=I, e=DK)
                             ).then_inc(s_v, 1)

            def shift_high(u):
                F = NMF * u + NF
                act.wait_ge(s_smf, F + 1)
                if u >= 2:
                    act.wait_ge(s_sh[u % 2], 32 * (u // 2))
                act.mul(SH[:, u % 2, :], SM[F % NSM][0:8 * I, 0:P], -1.0).then_inc(s_hi, 1)

            def exp(u, n):
                F = NF * u + n
                c, j0, m = FILLS[n]
                i = I - c
                act.wait_ge(s_saf, F + 1)
                if I * u + i >= 2:
                    act.wait_ge(s_pv, I * u + i - 1)
                act.activation(PR[:, i % 2, j0:j0 + m, 0:SUB * c],
                               att_bank(u, n)[:, 0:m * SUB * c].rearrange("p (j w) -> p j w", j=m),
                               ACT.Exp, scale=SCALE).then_inc(s_exp, 1)

            def copy_pv(u):
                act.wait_ge(s_pv, I * (u + 1))
                if u >= 4:
                    act.wait_ge(s_otp, T * (u // 2 - 1))
                act.copy(OT[:, (u // 2) % 2, u % 2, :], PV[:, :]).then_inc(s_ot, 1)

            def copy_pv_half(half):
                u, q = NU - 1, slice(S // 2 * half, S // 2 * (half + 1))
                act.wait_ge(s_pv, I * u + I // 2 * (half + 1))
                act.wait_ge(s_otp, T * (u // 2 - 1))
                act.copy(OT[:, (u // 2) % 2, u % 2, q], PV[:, q]).then_inc(s_ot, 1)

            def copy_turned(b, part, ready, done):
                act.wait_ge(ready, tiles(b, part))
                t = slice(part[0], part[0] + part[1])
                act.copy(FT[:, b, t, :].rearrange("p t n -> p (t n)"),
                         post_bank(b, part)[:, P * t.start:P * t.stop]).then_inc(done, part[1])

            def top_exp(b, part=WHOLE[0]):
                act.wait_ge(s_df, turn(b, part) + 1)
                t = slice(part[0], part[0] + part[1])
                act.activation(E1[:, b, t], DF[:, b, t], ACT.Exp).then_inc(s_e1, 1)

            def weigh_hi(b, t, half):
                n = T * b + t
                act.wait_ge(s_mep[1], n + 1)
                act.wait_ge(s_g, tiles(b, WHOLE[0]) if b < B - 1 else tiles(b, HALVES[t // 2]))
                if n >= 2 and (b < B - 1 or t < 2):
                    act.wait_ge(s_o[n % 2], n // 2)
                for e in range(2 * half, 2 * half + 2):
                    last = act.activation(products(b, t)[:, 4 + e, :], expert_bank(b, 2 * t + 1)[:, e * DO:(e + 1) * DO], ACT.Copy,
                                          scale=G[:, b, t, 4 + e:5 + e])
                if half:
                    last.then_inc(s_me[1], 1)

            act.wait_ge(s_wq, 16 * 5)
            act.copy(WP[:, :].rearrange("k (e s p) -> k p s e", s=2, p=NP),
                     Wu[:, 0, :].rearrange("k (p s e) -> k p s e", s=2, e=DK)).then_inc(s_wp, 1)
            act.wait_ge(s_wdp, 1)
            act.copy(WdT[:, :], MB[0:2 * C, 0:P]).then_inc(s_wd, 1)
            act.wait_ge(s_wfp, 3)
            act.copy(WF[:, 0, :], SM[1][:, 0:P]).then_inc(s_wf, 1)
            act.copy(WF[:, 1:3, :].rearrange("p n m -> p (n m)"), MB[:, P:3 * P]).then_inc(s_wf, 1)
            copy_xT(0)
            part1(0, 0)
            part1(0, 1)
            act.wait_ge(s_be, 16)
            act.copy(BP[:, 0, :], BE[:, :]).then_inc(s_b, 1)
            copy_v(0)
            for u in range(-1, NU + 1):
                for n in range(NF if u < NU else LAG):
                    now = NF * (u + 1) + n
                    a = NF * u + n - LAG
                    if a >= 0:
                        exp(a // NF, a % NF)
                    if a >= NF and a % NF == 0:
                        copy_pv(a // NF - 1)
                    if a == NF * (NU - 1) + 17:
                        copy_pv_half(0)
                    if u == NU and n == LAG - 1:
                        copy_turned(B - 1, HALVES[0], s_ontp, s_ont)
                    for r in due("onT", now, LATE["onT"]):
                        copy_turned(r, WHOLE[0], s_ontp, s_ont)
                    for r in due("x2T", now, LATE["x2T"]):
                        copy_turned(r, WHOLE[0], s_x2tp, s_x2t)
                    for r in due("top", now):
                        top_exp(r)
                    for r in due("xT", now, LATE["xT"]):
                        copy_xT(r)
                    for r in due("q", now, LATE["q"]):
                        part1(r, 0)
                    for r in due("k", now, LATE["k"]):
                        part1(r, 1)
                    for r in due("v", now, LATE["v"]):
                        copy_v(r)
                    for r, k in experts_due(now, LATE["hi"]):
                        if k % 2:
                            weigh_hi(r, k // 2, 0)
                    for r, k in experts_due(now, LATE["hi2"]):
                        if k % 2:
                            weigh_hi(r, k // 2, 1)
                if u + 1 < NU:
                    shift_high(u + 1)
            copy_pv_half(1)
            b = B - 1
            copy_turned(b, HALVES[0], s_x2tp, s_x2t)
            copy_turned(b, HALVES[1], s_ontp, s_ont)
            top_exp(b, HALVES[0])
            copy_turned(b, HALVES[1], s_x2tp, s_x2t)
            weigh_hi(b, 0, 0)
            weigh_hi(b, 0, 1)
            weigh_hi(b, 1, 0)
            top_exp(b, HALVES[1])
            weigh_hi(b, 1, 1)
            weigh_hi(b, 2, 0)
            weigh_hi(b, 2, 1)
            weigh_hi(b, 3, 0)
            weigh_hi(b, 3, 1)

        @block.vector
        def _(dve):
            def stats(k, b, part=WHOLE[0]):
                ts = range(part[0], part[0] + part[1])
                for t in ts:
                    dve.bn_stats(ST6[:, k, b, t, :], X[:, b, t, :]).then_inc(s_st[k], 1)

            def variance(k, b, part=WHOLE[0]):
                ts = range(part[0], part[0] + part[1])
                dve.wait_ge(s_st[k], tiles(b, part))
                for t in ts:
                    dve.bn_aggr(MV[:, k, b, t, :], ST6[:, k, b, t, :]).then_inc(s_mv[k], 1)
                dve.wait_ge(s_mv[k], tiles(b, part))
                dve.tensor_scalar(VE[:, k, b, ts.start:ts.stop], MV[:, k, b, ts.start:ts.stop, 1], EPS, None,
                                  ALU.add).then_inc(s_ve[k], part[1])

            def norm(k, b, part=WHOLE[0]):
                stats(k, b, part)
                variance(k, b, part)

            def norm_out(k, b, part=WHOLE[0]):
                dve.wait_ge(s_rs[k], tiles(b, part))
                for t in range(part[0], part[0] + part[1]):
                    dve.tensor_scalar(TOK[:, b, t, :], X[:, b, t, :], MV[:, k, b, t, 0:1],
                                      RS[:, k, b, t:t + 1], ALU.subtract, ALU.mult).then_inc(s_ln[k], 1)

            def zero_rows(pieces):
                for n in pieces:
                    o, h = (0, 2 * n) if n < H // 2 else (1, 2 * n - H)
                    dve.memset((QS, KS)[o][0:64, 0, h:h + 2, :].rearrange("p h n -> p (h n)").bitcast(U32),
                               0).then_inc(s_zero[0], 1)

            def rest(b, o):
                dve.wait_ge(s_p1[o], b + 1)
                if b >= 2:
                    dve.wait_ge(s_qs[b % 2], stacked(b - 2))
                dve.tensor_tensor(RES[:, b % 2, o, :], qk_bank(b, o)[:, :], PT1[:, b % 2, o, :],
                                  ALU.subtract).then_inc(s_r[o], 1)
                dve.wait_ge(s_r[o], b + 1)
                dve.tensor_copy(PT2[:, b % 2, o, :], RES[:, b % 2, o, :]).then_inc(s_p2[o], 1)

            def maxima(u, n):
                F = NMF * u + n
                c, j0, m = FILLS[n]
                dve.wait_ge(s_smf, F + 1)
                if n == 0 and u >= 2:
                    dve.wait_ge(s_smf, NMF * (u - 1))
                dve.tensor_reduce(MX[:, u % 2, j0:j0 + m, c - 1],
                                  SM[F % NSM][:, 0:m * SUB * c].rearrange("p (j w) -> p j w", j=m),
                                  AX.X, ALU.max).then_inc(s_smr, 1)

            def shift_low(u):
                F = NMF * u + NF
                dve.wait_ge(s_hi, u + 1)
                dve.scalar_tensor_tensor(out=SH[4 * I:, u % 2, :], in0=SM[F % NSM][4 * I:8 * I, 0:P], scalar=-1.0,
                                         in1=SH[4 * I:, u % 2, :], op0=ALU.mult, op1=ALU.subtract
                                         ).then_inc(s_smr, 1)

            def normalise(b, half):
                k = 2 * b + half
                dve.wait_ge(s_otp, tiles(b, HALVES[half]))
                o = post_bank(b, HALVES[half])[:, :].rearrange("p (a c) -> p a c", c=32)
                dve.reciprocal(RL[:, b, half, :, :], o[:, :, 2 * DK:2 * DK + 2]).then_inc(s_rl, 1)
                dve.wait_ge(s_rl, k + 1)
                dve.tensor_tensor(
                    TOK[:, b, 2 * half:2 * half + 2, :].rearrange("p t (a s e) -> p (t a) s e", s=2, e=DK),
                    o[:, :, 0:2 * DK].rearrange("p a (s e) -> p a s e", s=2),
                    RL[:, b, half, :, :].unsqueeze(3).to_broadcast([P, 16, 2, DK]), ALU.mult).then_inc(s_on, 2)

            def residual(b, part=WHOLE[0]):
                dve.wait_ge(s_yp, tiles(b, part))
                t = slice(part[0], part[0] + part[1])
                xb = X[:, b, t, :].rearrange("p t d -> p (t d)")
                dve.tensor_tensor(xb, post_bank(b, part)[:, D * t.start:D * t.stop], xb, ALU.add).then_inc(s_x1, part[1])
                dve.wait_ge(s_x1, tiles(b, part))

            def router(b, part=WHOLE[0]):
                nt = part[1]
                ts = slice(part[0], part[0] + nt)
                if b == 0:
                    dve.wait_ge(s_w, 16 * 4)
                dve.wait_ge(s_lgp, tiles(b, part))
                dve.tensor_tensor(LG[:, b, ts, :],
                                  post_bank(b, part)[:, NE * ts.start:NE * ts.stop].rearrange("p (t e) -> p t e", t=nt),
                                  BG[:, :].unsqueeze(1).to_broadcast([P, nt, NE]), ALU.add).then_inc(s_lg, nt)
                dve.wait_ge(s_lg, tiles(b, part))
                for t in range(ts.start, ts.stop):
                    dve.max(TOP[:, b, t, :], LG[:, b, t, :]).then_inc(s_top, 1)
                dve.wait_ge(s_top, tiles(b, part))
                dve.tensor_tensor(DF[:, b, ts], TOP[:, b, ts, 1], TOP[:, b, ts, 0], ALU.subtract).then_inc(s_df, 1)

            def router_index(b, part=WHOLE[0]):
                nt = part[1]
                ts = slice(part[0], part[0] + nt)
                for t in range(ts.start, ts.stop):
                    dve.max_index(TIX[:, b, t, :], TOP[:, b, t, :], LG[:, b, t, :]).then_inc(s_tix, 1)
                dve.wait_ge(s_tix, tiles(b, part))
                dve.tensor_copy(TIF[:, b, ts, :], TIX[:, b, ts, 0:2]).then_inc(s_gate, 1)
                dve.wait_ge(s_const, 11)
                dve.wait_ge(s_gate, 8 * turn(b, part) + 1)
                for k in range(2):
                    dve.tensor_tensor(OH[:, b, k, ts, :], iota8[:, :].unsqueeze(1).to_broadcast([P, nt, NE]),
                                      TIF[:, b, ts, k].unsqueeze(2).to_broadcast([P, nt, NE]),
                                      ALU.is_equal).then_inc(s_gate, 1)

            def gates(b, part=WHOLE[0]):
                ts = slice(part[0], part[0] + part[1])
                done = 8 * turn(b, part)
                dve.wait_ge(s_e1, turn(b, part) + 1)
                dve.tensor_scalar(DEN[:, b, ts], E1[:, b, ts], 1.0, None, ALU.add).then_inc(s_gate, 1)
                dve.wait_ge(s_gate, done + 4)
                dve.reciprocal(G12[:, b, 0, ts], DEN[:, b, ts]).then_inc(s_gate, 1)
                dve.wait_ge(s_gate, done + 5)
                dve.tensor_tensor(G12[:, b, 1, ts], E1[:, b, ts], G12[:, b, 0, ts], ALU.mult).then_inc(s_gate, 1)

            def spread_gates(b, part=WHOLE[0]):
                nt = part[1]
                ts = slice(part[0], part[0] + nt)
                done = 8 * turn(b, part)
                dve.wait_ge(s_gate, done + 6)
                for k in range(2):
                    dve.tensor_tensor(GW[:, b, k, ts, :], OH[:, b, k, ts, :],
                                      G12[:, b, k, ts].unsqueeze(2).to_broadcast([P, nt, NE]),
                                      ALU.mult).then_inc(s_gate, 1)
                dve.wait_ge(s_gate, done + 8)
                dve.tensor_tensor(G[:, b, ts, :], GW[:, b, 0, ts, :], GW[:, b, 1, ts, :], ALU.add).then_inc(s_g, nt)

            def bias_parts():
                dve.wait_ge(s_b, 1)
                dve.tensor_tensor(BR[:, :], BE[:, :], BP[:, 0, :], ALU.subtract).then_inc(s_b, 1)
                dve.wait_ge(s_b, 2)
                dve.tensor_copy(BP[:, 1, :], BR[:, :]).then_inc(s_b, 1)
                dve.wait_ge(s_b, 3)
                dve.tensor_tensor(BE[:, :], BR[:, :], BP[:, 1, :], ALU.subtract).then_inc(s_b, 1)
                dve.wait_ge(s_b, 4)
                dve.tensor_copy(BP[:, 2, :], BE[:, :]).then_inc(s_b, 1)

            def weigh_lo(b, t):
                n = T * b + t
                dve.wait_ge(s_mep[0], n + 1)
                dve.wait_ge(s_g, tiles(b, WHOLE[0]) if b < B - 1 else tiles(b, HALVES[t // 2]))
                if n >= 2 and (b < B - 1 or t < 2):
                    dve.wait_ge(s_o[n % 2], n // 2)
                dve.tensor_tensor(products(b, t)[:, 0:4, :], expert_bank(b, 2 * t)[:, :].rearrange("p (e o) -> p e o", e=4),
                                  G[:, b, t, 0:4].unsqueeze(2).to_broadcast([P, 4, DO]),
                                  ALU.mult).then_inc(s_me[0], 1)

            def expert_sums(b, t):
                n = T * b + t
                pr, v = products(b, t), n // 2
                dve.wait_ge(s_me[0], n + 1)
                dve.wait_ge(s_me[1], n + 1)
                dve.tensor_tensor(pr[:, 0:4, :], pr[:, 0:4, :], pr[:, 4:8, :], ALU.add).then_inc(s_sum[1], 1)
                dve.wait_ge(s_sum[1], 3 * v + 1)
                dve.tensor_tensor(pr[:, 0:2, :], pr[:, 0:2, :], pr[:, 2:4, :], ALU.add).then_inc(s_sum[1], 1)
                dve.wait_ge(s_sum[1], 3 * v + 2)
                dve.tensor_tensor(pr[:, 0, :], pr[:, 0, :], pr[:, 1, :], ALU.add).then_inc(s_sum[1], 1)
                dve.wait_ge(s_sum[1], 3 * v + 3)
                dve.tensor_tensor(TOK[:, b, t, :], pr[:, 0, :], X[:, b, t, :], ALU.add).then_inc(s_o[1], 1)

            zero_rows(range(0, 5))
            dve.wait_ge(s_x[0], 16)
            norm(0, 0)
            zero_rows(range(5, 7))
            norm_out(0, 0)
            zero_rows(range(7, (H + ZEROED) // 2))
            for o in range(2):
                rest(0, o)
            for o in range(2):
                dve.wait_ge(s_p2[o], 1)
                dve.tensor_tensor(PT3[:, 0, o, :], RES[:, 0, o, :], PT2[:, 0, o, :], ALU.subtract).then_inc(s_p3[o], 1)
            bias_parts()
            for u in range(-1, NU):
                for n in range(NF):
                    now = NF * (u + 1) + n
                    if u + 1 < NU:
                        maxima(u + 1, n)
                    for r, k in experts_due(now, LATE["lo"]):
                        if k % 2 == 0:
                            weigh_lo(r, k // 2)
                    for r in due("oT0", now, LATE["oT0"]):
                        normalise(r, 0)
                    for r in due("oT1", now, LATE["oT1"]):
                        normalise(r, 1)
                    for r in due("y", now, LATE["y"]):
                        residual(r)
                    for r in due("ln2", now, LATE["y"]):
                        stats(1, r)
                    for r in due("ln2_var", now, LATE["y"]):
                        variance(1, r)
                    for r in due("ln2_out", now):
                        norm_out(1, r, HALVES[0])
                    for r in due("ln2_out2", now):
                        norm_out(1, r, HALVES[1])
                    for r in due("logits", now, LATE["logits"]):
                        router(r)
                    for r in due("index", now, LATE["logits"]):
                        router_index(r)
                    for r in due("gates", now):
                        gates(r)
                    for r in due("gates2", now):
                        spread_gates(r)
                    for r in due("ln1", now):
                        dve.wait_ge(s_x[r], 16)
                        stats(0, r)
                    for r in due("ln1_var", now):
                        variance(0, r)
                    for r in due("ln1_out", now):
                        norm_out(0, r, HALVES[0])
                    for r in due("ln1_out2", now):
                        norm_out(0, r, HALVES[1])
                    for r in due("q", now, LATE["q_rest"]):
                        rest(r, 0)
                    for r in due("k", now, LATE["k_rest"]):
                        rest(r, 1)
                if u + 1 < NU:
                    shift_low(u + 1)
            b = B - 1
            normalise(b, 0)
            residual(b, HALVES[0])
            norm(1, b, HALVES[0])
            normalise(b, 1)
            norm_out(1, b, HALVES[0])
            residual(b, HALVES[1])
            norm(1, b, HALVES[1])
            router(b, HALVES[0])
            norm_out(1, b, HALVES[1])
            router_index(b, HALVES[0])
            gates(b, HALVES[0])
            spread_gates(b, HALVES[0])
            weigh_lo(b, 0)
            router(b, HALVES[1])
            weigh_lo(b, 1)
            router_index(b, HALVES[1])
            gates(b, HALVES[1])
            spread_gates(b, HALVES[1])
            weigh_lo(b, 2)
            weigh_lo(b, 3)
            expert_sums(b, 1)
            expert_sums(b, 3)


_INS = ["L0_attn_x", "L0_attn_W_dq", "L0_attn_W_uq", "L0_attn_W_dkv", "L0_attn_W_uk", "L0_attn_W_uv",
        "L0_attn_W_o", "L0_ffn_We", "L0_ffn_be", "L0_ffn_Wg", "L0_ffn_bg"]


def kernel(**inputs):
    import numpy as _np
    import concourse.bacc as _bacc
    from concourse import mybir as _mybir
    from concourse.bass_utils import run_bass_kernel_spmd as _run

    nc = _bacc.Bacc("TRN2", target_bir_lowering=False, num_devices=1)
    arrays, args = {}, []
    for name in _INS:
        a = _np.ascontiguousarray(inputs[name])
        arrays[f"in_{name}_dram"] = a
        args.append(nc.dram_tensor(f"in_{name}_dram", a.shape, _mybir.dt.from_np(a.dtype), kind="ExternalInput").ap())
    shape = inputs["L0_attn_x"].shape
    args.append(nc.dram_tensor("out_0_dram", shape, _mybir.dt.float32, kind="ExternalOutput").ap())
    build(nc, *args)
    r = _run(nc, [arrays], core_ids=[0])
    return r.results[0]["out_0_dram"]
```
